# Optimizing a Trainium2 kernel written in Bass

```python
import numpy as np
import jax
import jax.numpy as jnp

def _softmax(x, axis=-1):
    return jax.nn.softmax(x, axis=axis)
def _gelu(x):
    return jax.nn.gelu(x, approximate=True)
def _silu(x):
    return jax.nn.silu(x)
def _sigmoid(x):
    return jax.nn.sigmoid(x)
def _layernorm(x, axis=-1, eps=1e-5):
    m = jnp.mean(x, axis=axis, keepdims=True)
    v = jnp.var(x, axis=axis, keepdims=True)
    return (x - m) / jnp.sqrt(v + eps)
def _scatter_add(tgt, idx, src, axis=0):
    return tgt.at[idx].add(src)
def _segment_sum(src, seg, n):
    return jax.ops.segment_sum(src, seg, n)

kernel_name = 'mk_adj_preln_d2_adj_512_8e5f2c'

def setup_inputs(seed: int = 0):
    np.random.seed(seed)
    _w = jnp.asarray
    def _rec_inputs():
        import jax
        import jax.numpy as jnp
        _gk = jax.random.key(seed)
        x = -0.0005207 + 1.001 * jax.random.normal(jax.random.fold_in(_gk, 1), (4096, 512), jnp.float32)
        _a = jax.random.bernoulli(jax.random.fold_in(_gk, 2), 0.00195312, (4096, 4096))
        _a = jnp.logical_or(_a, jnp.swapaxes(_a, -1, -2))
        _a = jnp.logical_or(_a, jnp.eye(4096, dtype=bool))
        adj = _a.astype(jnp.int32)
        return x, adj
    x, adj = _rec_inputs()
    def _L0_gnn_setup():
        import jax, jax.numpy as jnp
        import numpy as np
        HEAD_SIZE = 8
        QK_DIM = 512
        V_DIM = 512
        N = 4096
        ATT_DIM = QK_DIM // HEAD_SIZE
        SCALE = ATT_DIM ** (-0.5)
        NEG_FILL = jnp.float32(-9000000000000000.0)
        key = jax.random.key(seed)
        k1, k2, k3, k4 = jax.random.split(key, 4)
        x1 = jax.random.normal(k1, (N, QK_DIM), dtype=jnp.float32)
        x2 = jax.random.normal(k2, (N, QK_DIM), dtype=jnp.float32)
        v = jax.random.normal(k3, (N, V_DIM), dtype=jnp.float32)
        adj = jax.random.randint(k4, (N, N), 0, 2, dtype=jnp.int32)
        return {'x1': x1, 'x2': x2, 'v': v, 'adj': adj}
    _L0_gnn_all = _L0_gnn_setup()
    _L0_gnn_in = {k: v for k, v in _L0_gnn_all.items() if k in ('x2', 'v', )}
    del _L0_gnn_all

    def _L1_gnn_setup():
        import jax, jax.numpy as jnp
        import numpy as np
        N, F, FP, K = (4096, 512, 64, 8)
        ALPHA = 0.2
        NEG_INF = -1e+16
        key = jax.random.key(seed)
        k1, k2, k3, k4 = jax.random.split(key, 4)
        gain = np.sqrt(2.0 / (1.0 + ALPHA ** 2))
        node_matrix = jax.random.normal(k1, (N, F), dtype=jnp.float32)
        adjacency_matrix = jax.random.randint(k2, (N, N), 0, 2, dtype=jnp.int32)
        W = jax.random.normal(k3, (K, F, FP), dtype=jnp.float32) * (gain * np.sqrt(2.0 / (F + FP)))
        a = jax.random.normal(k4, (K, 2 * FP, 1), dtype=jnp.float32) * (gain * np.sqrt(2.0 / (2 * FP + 1)))
        return {'node_matrix': node_matrix, 'adjacency_matrix': adjacency_matrix, 'W': W, 'a': a}
    _L1_gnn_all = _L1_gnn_setup()
    _L1_gnn_in = {k: v for k, v in _L1_gnn_all.items() if k in ('W', 'a', )}
    del _L1_gnn_all

    return {
        "x": x,
        "adj": adj,
        "L0_gnn_x2": _L0_gnn_in["x2"],
        "L0_gnn_v": _L0_gnn_in["v"],
        "L1_gnn_W": _L1_gnn_in["W"],
        "L1_gnn_a": _L1_gnn_in["a"],
    }

def reference(x, adj, L0_gnn_x2, L0_gnn_v, L1_gnn_W, L1_gnn_a):
    import jax
    import jax.numpy as jnp
    def _L0_gnn_ref(x1, x2, v, adj):
        import jax, jax.numpy as jnp
        import numpy as np
        HEAD_SIZE = 8
        QK_DIM = 512
        V_DIM = 512
        N = 4096
        ATT_DIM = QK_DIM // HEAD_SIZE
        SCALE = ATT_DIM ** (-0.5)
        NEG_FILL = jnp.float32(-9000000000000000.0)
        n = x1.shape[0]
        q = x1.reshape(n, HEAD_SIZE, -1).transpose(1, 0, 2) * SCALE
        k = x2.reshape(n, HEAD_SIZE, -1).transpose(1, 0, 2)
        vv = v.reshape(n, HEAD_SIZE, -1).transpose(1, 0, 2)
        scores = jnp.einsum('hnd,hmd->hnm', q, k)
        scores = jnp.where(adj > 0, scores, NEG_FILL)
        attn = jax.nn.softmax(scores, axis=-1)
        out = jnp.einsum('hnm,hmd->hnd', attn, vv)
        return out.transpose(1, 0, 2).reshape(n, -1)

    def _L1_gnn_ref(node_matrix, adjacency_matrix, W, a):
        import jax, jax.numpy as jnp
        import numpy as np
        N, F, FP, K = (4096, 512, 64, 8)
        ALPHA = 0.2
        NEG_INF = -1e+16
        h = jnp.einsum('nf,kfp->knp', node_matrix, W)
        a_src = a[:, :FP, 0]
        a_dst = a[:, FP:, 0]
        f1 = jnp.einsum('knp,kp->kn', h, a_src)
        f2 = jnp.einsum('knp,kp->kn', h, a_dst)
        e = jax.nn.leaky_relu(f2[:, :, None] + f1[:, None, :], negative_slope=ALPHA)
        e = jnp.where(adjacency_matrix[None, :, :] > 0, e, NEG_INF)
        att = jax.nn.softmax(e, axis=-1)
        out = jnp.einsum('knm,kmp->knp', att, h)
        return jnp.transpose(out, (1, 0, 2)).reshape(N, K * FP)

    h = jnp.maximum(_layernorm(x, axis=-1), 0.0)
    x = x + _L0_gnn_ref(h, L0_gnn_x2, L0_gnn_v, adj)
    h = jnp.maximum(_layernorm(x, axis=-1), 0.0)
    x = x + _L1_gnn_ref(h, adj, L1_gnn_W, L1_gnn_a)
    return x


_drawn_inputs = setup_inputs


def setup_inputs(seed=0):
    import zlib

    import numpy as np

    out = dict(_drawn_inputs(seed))
    spreads = {}
    factors = {}
    for name, (base, spread) in spreads.items():
        noise = np.random.default_rng([zlib.crc32(name.encode()), seed]).standard_normal(out[name].shape)
        drawn = base * np.exp(spread * noise) if base else spread * noise
        out[name] = jnp.asarray(drawn.astype(out[name].dtype))
    for name, factor in factors.items():
        out[name] = (out[name] * factor).astype(out[name].dtype)
    return out
```

```python
from contextlib import ExitStack

import concourse.bass as bass
from concourse import mybir
from concourse.alu_op_type import AluOpType as ALU

ACT = mybir.ActivationFunctionType
F32 = mybir.dt.float32
F32R = mybir.dt.float32r
BF16 = mybir.dt.bfloat16
I32 = mybir.dt.int32
AX = mybir.AxisListType

P = 128
N = 4096
D = 512
H = 8
DH = D // H
NT = N // P
PAIRS = H // 2
SUB = 2
GROUPS = NT // SUB
UNITS = H * GROUPS
V_ALL = UNITS * SUB
BLK = 16
CH = N // P
NEG = -float(2 ** 53)
LOWEST = -3.0e38
EPS = 1e-5
SCALE = DH ** -0.5
ALPHA = 0.2


class Unit:

    def __init__(self, loop, j, made=False):
        self.loop, self.j, self.made = loop, j, made
        self.fixed = loop + j if isinstance(loop, int) else None

    def at(self, a, b):
        if self.fixed is not None:
            return a * self.fixed + b
        return self.loop * a + (a * self.j + b)

    def exists(self, shift=0):
        return self.fixed is None or 0 <= self.fixed + shift < UNITS

    def has_tile(self, c):
        return self.fixed is None or 0 <= 2 * self.fixed + c < V_ALL


def normalise(nc, eng, s, bufs):
    x_all, st, mean, work, rstd = bufs
    for c in range(4):
        eng.wait_ge(s["x_in"][c], 16)
    with eng.Fori(0, NT) as t:
        nc.vector.bn_stats(st[:, t, :], x_all[:, t, :]).then_inc(s["stats"], 1)
    eng.wait_ge(s["stats"], NT)
    n = [0]

    def link(ins):
        n[0] += 1
        ins.then_inc(s["norm"], 1)
        eng.wait_ge(s["norm"], n[0])

    me, ve, mo, vo = (st[:, :, i] for i in (1, 2, 4, 5))
    link(nc.vector.tensor_tensor(mean[:], me, mo, ALU.add))
    link(nc.vector.tensor_scalar(mean[:], mean[:], 0.5, None, ALU.mult))
    link(nc.vector.tensor_tensor(work[:, 0, :], me, mo, ALU.subtract))
    link(nc.vector.tensor_tensor(work[:, 1, :], work[:, 0, :], work[:, 0, :], ALU.mult))
    link(nc.vector.tensor_tensor(work[:, 2, :], ve, vo, ALU.add))
    link(nc.vector.tensor_scalar(work[:, 3, :], work[:, 2, :], 1.0 / D, EPS, ALU.mult, ALU.add))
    nc.vector.scalar_tensor_tensor(out=work[:, 4, :], in0=work[:, 1, :], scalar=0.25, in1=work[:, 3, :],
                                   op0=ALU.mult, op1=ALU.add).then_inc(s["var"], 1)
    eng.wait_ge(s["std"], 1)
    nc.vector.reciprocal(rstd[:], work[:, 5, :]).then_inc(s["rstd"], 1)
    eng.wait_ge(s["rstd"], 1)


def prepare0(nc, x, x2, q_dram, k_dram, ident, make_ident, sem):
    with ExitStack() as ctx:
        sb = lambda name, shape, dt: ctx.enter_context(nc.sbuf_tensor(name, shape, dt))
        x_all = sb("a_x_all", [P, NT, D], F32)
        st = sb("a_st", [P, NT, 6], F32)
        mean = sb("a_mean", [P, NT], F32)
        work = sb("a_work", [P, 6, NT], F32)
        rstd = sb("a_rstd", [P, NT], F32)
        xn = sb("a_xn", [P, 2, D], F32)
        hq = sb("a_hq", [P, 2, D], F32)
        kx = sb("a_kx", [P, 2, D], F32)
        q_st = sb("a_q_st", [P, 2, PAIRS, 2, P], F32R)
        k_st = sb("a_k_st", [P, 2, PAIRS, 2, P], F32R)
        tq = ctx.enter_context(nc.psum_tensor("a_tq", [P, 2, D], F32))
        tk = ctx.enter_context(nc.psum_tensor("a_tk", [P, 2, D], F32))
        s = {n: sem("a_" + n) for n in ("stats", "norm", "var", "std", "rstd", "xn", "h", "tq", "tk", "q_hi",
                                        "q_lo", "k_hi", "k_lo",
                                        "passed_pool")}
        s["x_in"] = [sem(f"a_x_in{c}") for c in range(4)]
        k_in = [sem(f"a_k_in{r}") for r in range(2)]
        q_out = [sem(f"a_q_out{r}") for r in range(2)]
        k_out = [sem(f"a_k_out{r}") for r in range(2)]
        x_t = x.rearrange("(t p) d -> p t d", p=P)
        x2_t = x2.rearrange("(t p) d -> t p d", p=P)
        block = ctx.enter_context(nc.Block())

        def tiles(eng, body):
            for r in range(2):
                body(0, r, True)
            with eng.Fori(1, NT // 2) as i:
                for r in range(2):
                    body(i, r, False)

        @block.sync
        def _(sp):
            for c in range(4):
                sp.dma_start(x_all[:, 8 * c:8 * c + 8, :], x_t[:, 8 * c:8 * c + 8, :]).then_inc(s["x_in"][c], 16)

            def load(i, r, first):
                if not first:
                    sp.wait_ge(s["tk"], i * 2 + (r - 1))
                sp.dma_start(kx[:, r, :], x2_t[i * 2 + r]).then_inc(k_in[r], 16)

            tiles(sp, load)

        @block.gpsimd
        def _(pool):
            make_ident(pool)

            def store(i, r, first):
                pool.wait_ge(s["q_lo"], i * 2 + (r + 1))
                pool.sem_inc(s["passed_pool"], 1)
                pool.dma_start(q_dram[:, i * 2 + r, :, :, :].rearrange("a p b n -> p a b n"),
                               q_st[:, r].bitcast(F32)).then_inc(q_out[r], 16)
                pool.wait_ge(s["k_lo"], i * 2 + (r + 1))
                pool.sem_inc(s["passed_pool"], 1)
                for h2 in range(2):
                    for e in range(2):
                        dst = k_dram.rearrange("(a h) (b d) (t m) -> h b t d a m", h=2, b=2, m=P)[h2, e, i * 2 + r]
                        pool.dma_start(dst, k_st[DH * h2:DH * h2 + DH, r, :, e, :].bitcast(F32))\
                            .then_inc(k_out[r], 16)

            tiles(pool, store)
            for r in range(2):
                pool.wait_ge(q_out[r], 16 * (NT // 2))
                pool.wait_ge(k_out[r], 64 * (NT // 2))

        @block.vector
        def _(dve):
            normalise(nc, dve, s, (x_all, st, mean, work, rstd))

            def norm(i, r, first):
                if not first:
                    dve.wait_ge(s["h"], i * 2 + (r - 1))
                t = i * 2 + r
                nc.vector.tensor_scalar(xn[:, r, :], x_all[:, t, :], mean[:, bass.ds(t, 1)],
                                        rstd[:, bass.ds(t, 1)], ALU.subtract, ALU.mult).then_inc(s["xn"], 1)

            def low(i, r, first):
                dve.wait_ge(s["q_hi"], i * 2 + (r + 1))
                nc.vector.tensor_tensor(q_st[:, r, :, 1, :], tq[:, r].rearrange("p (a n) -> p a n", n=P),
                                        q_st[:, r, :, 0, :], ALU.subtract).then_inc(s["q_lo"], 1)
                dve.wait_ge(s["k_hi"], i * 2 + (r + 1))
                nc.vector.tensor_tensor(k_st[:, r, :, 1, :], tk[:, r].rearrange("p (a n) -> p a n", n=P),
                                        k_st[:, r, :, 0, :], ALU.subtract).then_inc(s["k_lo"], 1)

            tiles(dve, lambda i, r, first: (norm(i, r, first), low(i, r, first)))

        @block.scalar
        def _(act):
            act.wait_ge(s["var"], 1)
            nc.scalar.activation(work[:, 5, :], work[:, 4, :], ACT.Sqrt).then_inc(s["std"], 1)

            def body(i, r, first):
                act.wait_ge(s["xn"], i * 2 + (r + 1))
                if not first:
                    act.wait_ge(s["tq"], i * 2 + (r - 1))
                nc.scalar.activation(hq[:, r, :], xn[:, r, :], ACT.Relu, scale=SCALE).then_inc(s["h"], 1)
                act.wait_ge(s["tk"], i * 2 + (r + 1))
                if not first:
                    act.wait_ge(k_out[r], i * 64)
                nc.scalar.activation(k_st[:, r, :, 0, :], tk[:, r].rearrange("p (a n) -> p a n", n=P),
                                     ACT.Copy).then_inc(s["k_hi"], 1)
                act.wait_ge(s["tq"], i * 2 + (r + 1))
                if not first:
                    act.wait_ge(q_out[r], i * 16)
                nc.scalar.activation(q_st[:, r, :, 0, :], tq[:, r].rearrange("p (a n) -> p a n", n=P),
                                     ACT.Copy).then_inc(s["q_hi"], 1)

            tiles(act, body)

        @block.tensor
        def _(pe):
            pe.wait_ge(ident[1], 2)

            def body(i, r, first):
                pe.wait_ge(k_in[r], i * 16 + 16)
                if not first:
                    pe.wait_ge(s["k_lo"], i * 2 + (r - 1))
                for a in range(PAIRS):
                    mm = pe.transpose(tk[:, r, a * P:(a + 1) * P], kx[:, r, a * P:(a + 1) * P], ident[0][:])
                mm.then_inc(s["tk"], 1)
                pe.wait_ge(s["h"], i * 2 + (r + 1))
                if not first:
                    pe.wait_ge(s["q_lo"], i * 2 + (r - 1))
                for a in range(PAIRS):
                    mm = pe.transpose(tq[:, r, a * P:(a + 1) * P], hq[:, r, a * P:(a + 1) * P], ident[0][:])
                mm.then_inc(s["tq"], 1)

            tiles(pe, body)


def prepare1(nc, x1, w, a, v_dram, f_dram, f2, ident, sem):
    with ExitStack() as ctx:
        sb = lambda name, shape, dt: ctx.enter_context(nc.sbuf_tensor(name, shape, dt))
        x_all = sb("c_x_all", [P, NT, D], F32)
        st = sb("c_st", [P, NT, 6], F32)
        mean = sb("c_mean", [P, NT], F32)
        work = sb("c_work", [P, 6, NT], F32)
        rstd = sb("c_rstd", [P, NT], F32)
        w_sb = sb("c_w", [P, D // P, D], F32)
        a_bc = sb("c_a_bc", [P, 2, D], F32)
        xn = sb("c_xn", [P, 2, D], F32)
        hn = sb("c_hn", [P, 2, D], F32)
        ht = sb("c_ht", [P, 2, D], F32)
        hw_sb = sb("c_hw_sb", [P, 2, D], F32)
        prod = sb("c_prod", [P, 2, 2, D], F32)
        f1 = sb("c_f1", [P, H, NT], F32)
        f_rows = sb("c_f_rows", [P, 2, 2, P], F32)
        th = ctx.enter_context(nc.psum_tensor("c_th", [P, 2, D], F32))
        hw = ctx.enter_context(nc.psum_tensor("c_hw", [P, 2, D], F32))
        tf = ctx.enter_context(nc.psum_tensor("c_tf", [P, 2, P], F32))
        s = {n: sem("c_" + n) for n in ("stats", "norm", "var", "std", "rstd", "xn", "h", "th", "ht", "hw", "hw_sb",
                                        "prod", "f", "w_in", "a_in", "tf", "f_rows", "f_out", "f2")}
        s["x_in"] = [sem(f"c_x_in{c}") for c in range(4)]
        v_out = [sem(f"c_v_out{r}") for r in range(2)]
        x_t = x1.rearrange("(t p) d -> p t d", p=P)
        v_t = v_dram.rearrange("(t p) d -> t p d", p=P)
        block = ctx.enter_context(nc.Block())

        def tiles(eng, body):
            for r in range(2):
                body(0, r, True)
            with eng.Fori(1, NT // 2) as i:
                for r in range(2):
                    body(i, r, False)

        @block.sync
        def _(sp):
            for c in range(4):
                sp.dma_start(x_all[:, 8 * c:8 * c + 8, :], x_t[:, 8 * c:8 * c + 8, :]).then_inc(s["x_in"][c], 16)
            for c in range(D // P):
                sp.dma_start(w_sb[:, c, :].rearrange("p (k q) -> p k q", k=H),
                             w[:, c * P:(c + 1) * P, :].rearrange("k f q -> f k q")).then_inc(s["w_in"], 16)
            for e in range(2):
                src = a[:, e * DH:(e + 1) * DH, 0].unsqueeze(0).to_broadcast([P, H, DH])
                sp.dma_start(a_bc[:, e, :].rearrange("p (k q) -> p k q", k=H), src).then_inc(s["a_in"], 16)

            def store(i, r, first):
                sp.wait_ge(s["hw_sb"], i * 2 + (r + 1))
                sp.dma_start(v_t[i * 2 + r], hw_sb[:, r, :]).then_inc(v_out[r], 16)

            tiles(sp, store)
            sp.wait_ge(s["f_rows"], 2)
            for e in range(2):
                sp.dma_start(f_dram[e].rearrange("k (t n) -> (k t) n", n=P).rearrange("(j p) n -> p j n", p=P),
                             f_rows[:, e]).then_inc(s["f_out"], 16)
            sp.wait_ge(s["f_out"], 32)
            for r in range(2):
                sp.wait_ge(v_out[r], 16 * (NT // 2))

        @block.vector
        def _(dve):
            normalise(nc, dve, s, (x_all, st, mean, work, rstd))
            dve.wait_ge(s["a_in"], 32)

            def norm(i, r, first):
                if not first:
                    dve.wait_ge(s["h"], i * 2 + (r - 1))
                t = i * 2 + r
                nc.vector.tensor_scalar(xn[:, r, :], x_all[:, t, :], mean[:, bass.ds(t, 1)],
                                        rstd[:, bass.ds(t, 1)], ALU.subtract, ALU.mult).then_inc(s["xn"], 1)

            def dots(i, r, first):
                t = i * 2 + r
                dve.wait_ge(s["hw_sb"], i * 2 + (r + 1))
                if not first:
                    dve.wait_ge(s["f"], i * 4 + (2 * r - 2))
                for e in range(2):
                    nc.vector.tensor_tensor(prod[:, r, e, :], hw_sb[:, r, :], a_bc[:, e, :],
                                            ALU.mult).then_inc(s["prod"], 1)
                f2_v = f2[:].rearrange("p (a g h s) -> p a h g s", a=PAIRS, h=2, s=SUB)
                for e, dst in enumerate((f1[:, :, t], f2_v[:, :, :, i, r])):
                    dve.wait_ge(s["prod"], i * 4 + (2 * r + e + 1))
                    src = prod[:, r, e, :]
                    src = (src.rearrange("p (k q) -> p k q", k=H) if e == 0 else
                           src.rearrange("p (a h q) -> p a h q", a=PAIRS, h=2))
                    nc.vector.tensor_reduce(dst, src, AX.X, ALU.add).then_inc(s["f"], 1)

            tiles(dve, lambda i, r, first: (norm(i, r, first), dots(i, r, first)))
            dve.wait_ge(s["tf"], 1)
            nc.vector.tensor_copy(f_rows[:, 0], tf[:]).then_inc(s["f_rows"], 1)
            nc.vector.tensor_scalar(f_rows[:, 1], tf[:], ALPHA, None, ALU.mult).then_inc(s["f_rows"], 1)
            dve.wait_ge(s["f"], 2 * NT)
            nc.vector.tensor_scalar(f2[:], f2[:], 1.0 - ALPHA, None, ALU.mult).then_inc(s["f2"], 1)
            dve.wait_ge(s["f2"], 1)

        @block.scalar
        def _(act):
            act.wait_ge(s["var"], 1)
            nc.scalar.activation(work[:, 5, :], work[:, 4, :], ACT.Sqrt).then_inc(s["std"], 1)

            def body(i, r, first):
                act.wait_ge(s["xn"], i * 2 + (r + 1))
                if not first:
                    act.wait_ge(s["th"], i * 2 + (r - 1))
                nc.scalar.activation(hn[:, r, :], xn[:, r, :], ACT.Relu).then_inc(s["h"], 1)
                act.wait_ge(s["th"], i * 2 + (r + 1))
                if not first:
                    act.wait_ge(s["hw"], i * 2 + (r - 1))
                nc.scalar.activation(ht[:, r, :], th[:, r, :], ACT.Copy).then_inc(s["ht"], 1)
                act.wait_ge(s["hw"], i * 2 + (r + 1))
                if not first:
                    act.wait_ge(v_out[r], i * 16)
                    act.wait_ge(s["prod"], i * 4 + (2 * r - 2))
                nc.scalar.activation(hw_sb[:, r, :], hw[:, r, :], ACT.Copy).then_inc(s["hw_sb"], 1)

            tiles(act, body)

        @block.tensor
        def _(pe):
            pe.wait_ge(s["w_in"], 16 * (D // P))

            def body(i, r, first):
                pe.wait_ge(s["h"], i * 2 + (r + 1))
                if not first:
                    pe.wait_ge(s["ht"], i * 2 + (r - 1))
                for c in range(D // P):
                    mm = pe.transpose(th[:, r, c * P:(c + 1) * P], hn[:, r, c * P:(c + 1) * P], ident[0][:])
                mm.then_inc(s["th"], 1)
                pe.wait_ge(s["ht"], i * 2 + (r + 1))
                if not first:
                    pe.wait_ge(s["hw_sb"], i * 2 + (r - 1))
                for c in range(D // P):
                    mm = pe.matmul(hw[:, r, :], ht[:, r, c * P:(c + 1) * P], w_sb[:, c, :],
                                   start=(c == 0), stop=(c == D // P - 1))
                mm.then_inc(s["hw"], 1)

            tiles(pe, body)
            pe.wait_ge(s["f"], 2 * NT)
            for j in range(2):
                mm = pe.transpose(tf[:, j, :], f1[:].rearrange("p k t -> p (k t)")[:, j * P:(j + 1) * P], ident[0][:])
            mm.then_inc(s["tf"], 1)


def attend(nc, layer, x_in, x_out, v_dram, mask_dram, ident, stack2, sem, adj=None, q_dram=None, k_dram=None,
           f_dram=None, f2=None):
    name = "bd"[layer] + "_"
    AK = 8 if layer == 0 else 4
    AW = N // AK
    EK, EW = 4, N // 4
    ACT_EVAC = [b for b in range(BLK) if (b % 2 or layer == 1)]
    DVE_EVAC = [b for b in range(BLK) if b not in ACT_EVAC]
    with ExitStack() as ctx:
        sb = lambda n, shape, dt: ctx.enter_context(nc.sbuf_tensor(name + n, shape, dt))
        z = sb("z", [P, 4, N], F32)
        mask = sb("mask", [P, 4, N], BF16)
        v_sb = sb("v", [P, 2, CH, DH], F32)
        pt = sb("pt", [P, 4, 512], F32)
        o_sb = sb("o_sb", [P, 2, 2 * P], F32)
        res = sb("res", [P, 2, SUB, P], F32)
        mx = sb("mx", [P, 8, AK], F32)
        nm = sb("nm", [P, 8], F32)
        rs = sb("rs", [P, 8, EK], F32)
        rsum = sb("rsum", [P, 2, 2], F32)
        rinv = sb("rinv", [P, 2, 2], F32)
        if layer == 0:
            k_sb = sb("k", [P, 2, N], F32R)
            q_sb = sb("q", [P, 4, 2, P], F32R)
            adj_sb = sb("adj", [P, 2, N], I32)
        else:
            f_bc = sb("f_bc", [P, 2, 2, N], F32)
        t_ps = ctx.enter_context(nc.psum_tensor(name + "t_ps", [P, 4, 512], F32))
        o_ps = ctx.enter_context(nc.psum_tensor(name + "o_ps", [P, 2, 512], F32))
        s_ps = ctx.enter_context(nc.psum_tensor(name + "s_ps", [P, 2, 512], F32))

        s = {n: sem(name + n) for n in (
            "scores", "masked", "max", "exp", "leaky", "turned", "evac_act", "evac_dve", "pv", "o_copied", "o_turned",
            "added", "conv", "sums", "link", "passed_dve", "passed_act", "passed_pool")}
        mask_in = [sem(f"{name}mask_in{i}") for i in range(4)]
        mask_out = [sem(f"{name}mask_out{i}") for i in range(4)]
        q_in = [sem(f"{name}q_in{i}") for i in range(4)]
        key_in = [sem(f"{name}key_in{i}") for i in range(2)]
        v_in = [sem(f"{name}v_in{i}") for i in range(2)]
        adj_in = [sem(f"{name}adj_in{i}") for i in range(2)]
        res_in = [sem(f"{name}res_in{i}") for i in range(2)]
        res_out = [sem(f"{name}res_out{i}") for i in range(2)]
        x_g = x_in.rearrange("(g s p) d -> g p s d", s=SUB, p=P)
        y_g = x_out.rearrange("(g s p) d -> g p s d", s=SUB, p=P)
        v_c = v_dram.rearrange("(c p) d -> p c d", p=P)
        LAST = UNITS // 4 - 1
        if layer == 0:
            segments = [("static", -2, 4), ("loop", 1, 7), ("static", 28, 32), ("loop", 8, LAST),
                        ("static", 4 * LAST, UNITS + 1)]
        else:
            segments = [("static", -2, 4), ("loop", 1, LAST), ("static", 4 * LAST, UNITS + 1)]
        UP = 2 * GROUPS

        def f2_of(u, c):
            return f2[:, bass.ds(u.loop * 2 + (2 * u.j + c), 1)]

        def evac_wait(eng, u, b):
            du, b = divmod(b, BLK)
            if not u.exists(du):
                return
            which, own = ("evac_act", ACT_EVAC) if b in ACT_EVAC else ("evac_dve", DVE_EVAC)
            eng.wait_ge(s[which], u.at(len(own), len(own) * du + own.index(b) + 1))

        def walk(eng, body):
            for kind, a, b in segments:
                if kind == "static":
                    for n in range(a, b):
                        body(Unit(4 * (n // 4), n % 4))
                else:
                    with eng.Fori(a, b) as i:
                        for j in range(4):
                            body(Unit(i * 4, j, made=layer == 0 and a == 1))

        block = ctx.enter_context(nc.Block())

        @block.sync
        def _(sp):
            def load_keys(p, h2):
                if p:
                    last = 4 * GROUPS * p - (3 if h2 == 0 else 1)
                    if layer == 0:
                        sp.wait_ge(s["scores"], AK * (last + 1))
                    else:
                        sp.wait_ge(s["masked"], AK * (last + 1))
                if layer == 0:
                    sp.dma_start(k_sb[:, h2, :].bitcast(F32), k_dram[2 * p + h2]).then_inc(key_in[h2], 16)
                else:
                    for e in range(2):
                        sp.dma_start(f_bc[:, h2, e, :], f_dram[e, 2 * p + h2:2 * p + h2 + 1, :].to_broadcast([P, N]))\
                            .then_inc(key_in[h2], 16)

            def load_values(p, h2):
                if p:
                    sp.wait_ge(s["pv"], BLK * (UP * p - 1 + h2))
                col = (2 * p + h2) * DH
                sp.dma_start(v_sb[:, h2], v_c[:, :, col:col + DH]).then_inc(v_in[h2], 16)

            def load_queries(p, g, first=False):
                for i in range(4):
                    h2, sub = divmod(i, 2)
                    if not first:
                        sp.wait_ge(s["scores"], g * (4 * AK) + AK * (4 * GROUPS * p + i - 3))
                    src = q_dram[p, g * SUB + sub, DH * h2:DH * h2 + DH].rearrange("d b n -> d (b n)")
                    for half in range(2):
                        sp.dma_start(q_sb[DH * half:DH * half + DH, i].rearrange("d b n -> d (b n)").bitcast(F32),
                                     src).then_inc(q_in[i], 16)

            def load_masks(slot2, g, wait):
                for sub in range(SUB):
                    if wait is not None:
                        sp.wait_ge(s["masked"], wait)
                    sp.dma_start(mask[:, 2 * slot2 + sub, :], mask_dram[g * SUB + sub])\
                        .then_inc(mask_in[2 * slot2 + sub], 16)

            def load_adj(t, sub, first=False):
                if not first:
                    sp.wait_ge(s["conv"], t + (-1))
                sp.dma_start(adj_sb[:, sub, :], adj.rearrange("(t p) m -> t p m", p=P)[t]).then_inc(adj_in[sub], 16)

            def freed(p, g, gm):
                return g * (4 * AK) + AK * 4 * (GROUPS * p - 1) if gm else None

            if layer == 0:
                load_adj(0, 0, True)
                load_adj(1, 1, True)
                load_queries(0, 0, True)
                load_keys(0, 0)
                load_keys(0, 1)
                load_values(0, 0)
                load_values(0, 1)
            else:
                load_masks(0, 0, None)
                load_keys(0, 0)
                load_keys(0, 1)
                load_values(0, 0)
                load_values(0, 1)
                load_masks(1, 1, None)

            def step(p, g, parity, load_next_mask=True):
                if layer == 0 and p == 0:
                    for sub in range(SUB):
                        load_adj(g * 2 + (2 + sub), sub)
                elif load_next_mask:
                    load_masks(1 - parity, g + 1, g * (4 * AK) + 4 * AK * (GROUPS * p))
                if layer == 0:
                    load_queries(p, g + 1)

            for p in range(PAIRS):
                if p:
                    load_masks(1, 1, 4 * AK * GROUPS * p)
                    load_values(p, 0)
                    load_values(p, 1)
                    if layer == 0:
                        load_queries(p, 1)
                else:
                    step(0, 0, 0, load_next_mask=False)
                with sp.Fori(0, GROUPS // 2 - 1) as i:
                    step(p, i * 2 + 1, 1)
                    step(p, i * 2 + 2, 0)
                if p + 1 < PAIRS:
                    if layer == 0 and p == 0:
                        for i in range(4):
                            sp.wait_ge(mask_out[i], 16 * (GROUPS // 2))
                    load_masks(0, 0, 4 * AK * (GROUPS * (p + 1) - 1))
                    load_keys(p + 1, 0)
                    load_keys(p + 1, 1)
                    if layer == 0:
                        load_queries(p + 1, 0)

        @block.gpsimd
        def _(pool):
            def group(p, g, parity, first):
                big = g + GROUPS * p
                if not first:
                    pool.wait_ge(res_out[parity], (g - parity) * 8 + 8 * GROUPS * p)
                    pool.sem_inc(s["passed_pool"], 1)
                pool.dma_start(res[:, parity], x_g[g][:, :, P * p:P * p + P]).then_inc(res_in[parity], 16)
                if layer == 0 and p == 0:
                    for sub in range(SUB):
                        pool.wait_ge(s["conv"], g * 2 + (sub + 1))
                        pool.sem_inc(s["passed_pool"], 1)
                        pool.dma_start(mask_dram[g * SUB + sub], mask[:, 2 * parity + sub, :])\
                            .then_inc(mask_out[2 * parity + sub], 16)
                pool.wait_ge(s["added"], big * 2 + 2)
                pool.sem_inc(s["passed_pool"], 1)
                pool.dma_start(y_g[g][:, :, P * p:P * p + P], res[:, parity]).then_inc(res_out[parity], 16)

            for p in range(PAIRS):
                for parity in range(2):
                    group(p, parity, parity, p == 0)
                with pool.Fori(1, GROUPS // 2) as i:
                    for parity in range(2):
                        group(p, i * 2 + parity, parity, False)
            for parity in range(2):
                pool.wait_ge(res_out[parity], 8 * GROUPS * PAIRS)

        def mask_wait(eng, u, c):
            w = 2 * u.j + c
            slot = 2 * (w % 8 // 4) + w % 2
            if layer == 0 and (u.made if u.fixed is None else 2 * u.fixed + c < 4 * GROUPS):
                eng.wait_ge(s["conv"], u.loop + (2 * (w // 4) + w % 2 + 1))
            else:
                skip = GROUPS // 2 if layer == 0 else 0
                eng.wait_ge(mask_in[slot], u.loop * 4 + 16 * (w // 8 + 1 - skip))

        @block.tensor
        def _(pe):
            def body(u):
                for b in range(BLK):
                    if u.exists():
                        if b % 4 == 0:
                            pe.wait_ge(s["exp"], u.at(8, 5 + b // 4))
                        evac_wait(pe, u, b - 4)
                        for i in range(2):
                            for sub in range(SUB):
                                c = 2 * b + i
                                mm = pe.transpose(t_ps[:, b % 4, (2 * i + sub) * P:(2 * i + sub + 1) * P],
                                                  z[:, 2 * (u.j % 2) + sub, c * P:(c + 1) * P], ident[0][:])
                        mm.then_inc(s["turned"], 1)
                    if layer == 0:
                        c, k = (3, b) if b < 8 else (4, b - 8)
                        if u.has_tile(c):
                            v4 = (2 * u.j + c) % 4
                            h2 = v4 // 2
                            if k == 0:
                                pe.wait_ge(q_in[v4], u.loop * 16 + 32 * ((2 * u.j + c) // 4 + 1))
                                pe.wait_ge(key_in[h2], (u.at(1, c // 2) // UP) * 16 + 16)
                            if not (u.fixed is not None and 2 * u.fixed + c == 0 and k < 2):
                                pe.wait_ge(s["masked"], u.at(2 * AK, AK * c + k - 1))
                            for e in range(2):
                                mm = pe.matmul(s_ps[:, k % 2, :], q_sb[:, v4, e, :],
                                               k_sb[:, h2, k * AW:(k + 1) * AW], start=(e == 0), stop=(e == 1))
                            mm.then_inc(s["scores"], 1)
                    du, b2 = divmod(b - 3, BLK)
                    if u.exists(du):
                        h2 = (u.j + du) % 2
                        if b2 == 0:
                            pe.wait_ge(v_in[h2], (u.at(1, du) // UP) * 16 + 16)
                            if u.exists(du - 2):
                                pe.wait_ge(s["added"], u.at(1, du - 1))
                        evac_wait(pe, u, b - 3)
                        for i in range(2):
                            mm = pe.matmul(o_ps[DH * i:DH * i + DH, h2, 0:SUB * P], v_sb[:, h2, 2 * b2 + i, :],
                                           pt[:, b2 % 4, i * 256:(i + 1) * 256], start=(b2 == 0),
                                           stop=(b2 == BLK - 1))
                        mm.then_inc(s["pv"], 1)
                    if b == 5 and u.exists(-1):
                        h2 = (u.j - 1) % 2
                        pe.wait_ge(s["o_copied"], u.at(1, 0))
                        for sub in range(SUB):
                            mm = pe.matmul(o_ps[:, h2, 256 + DH * sub:256 + DH * sub + DH],
                                           o_sb[:, h2, sub * P:(sub + 1) * P], stack2[:], start=True, stop=True,
                                           skip_group_check=True)
                        mm.then_inc(s["o_turned"], 1)

            walk(pe, body)

        def copy_out(eng, u, b, own, done):
            du, b = divmod(b, BLK)
            if b not in own or not u.exists(du):
                return
            eng.wait_ge(s["turned"], u.at(BLK, BLK * du + b + 1))
            if not (u.fixed is not None and BLK * (u.fixed + du) + b < 4):
                eng.wait_ge(s["pv"], u.at(BLK, BLK * du + b - 3))
            if done == "evac_act":
                nc.scalar.activation(pt[:, b % 4, :], t_ps[:, b % 4, :], ACT.Copy).then_inc(s[done], 1)
            else:
                nc.vector.tensor_copy(pt[:, b % 4, :], t_ps[:, b % 4, :]).then_inc(s[done], 1)

        @block.vector
        def _(dve):
            def convert(tile, slot, sub, reuse):
                dve.wait_ge(adj_in[sub], tile_in(tile))
                if reuse is not None:
                    dve.wait_ge(mask_out[slot], reuse)
                nc.vector.tensor_scalar(mask[:, slot, :], adj_sb[:, sub, :], 0, NEG, ALU.is_le,
                                        ALU.mult).then_inc(s["conv"], 1)

            def tile_in(tile):
                return tile * 16 + 16

            def make_mask(u):
                sub = 0 if u.j % 2 else 1
                if u.fixed is not None:
                    g = (u.fixed + 3 - sub) // 2
                    if u.fixed < -2 or g >= GROUPS or (u.fixed == -2):
                        return
                    convert(g, 2 * (g % 2) + sub, sub, 16 * (g // 2) if g >= 2 else None)
                elif u.made:
                    dg = (u.j + 3 - sub) // 2
                    slot = 2 * (dg % 2) + sub
                    dve.wait_ge(adj_in[sub], u.loop * 8 + (16 * dg + 16))
                    dve.wait_ge(mask_out[slot], u.loop * 4 + 16 * (dg // 2))
                    nc.vector.tensor_scalar(mask[:, slot, :], adj_sb[:, sub, :], 0, NEG, ALU.is_le,
                                            ALU.mult).then_inc(s["conv"], 1)

            def leaky(u, c, k):
                if not u.has_tile(c):
                    return
                v8 = (2 * u.j + c) % 8
                h2 = (v8 // 2) % 2
                if k == 0:
                    dve.wait_ge(key_in[h2], (u.at(1, c // 2) // UP) * 32 + 32)
                if u.fixed is None or 2 * u.fixed + c >= 4:
                    dve.wait_ge(s["turned"], u.at(BLK, BLK * ((c - 4) // 2) + BLK // AK * (k + 1)))
                dve.sem_inc(s["passed_dve"], 1)
                cols = slice(k * AW, (k + 1) * AW)
                nc.vector.scalar_tensor_tensor(out=z[:, v8 % 4, cols], in0=f_bc[:, h2, 0, cols], scalar=f2_of(u, c),
                                               in1=f_bc[:, h2, 1, cols], op0=ALU.add,
                                               op1=ALU.max).then_inc(s["leaky"], 1)

            def masked(u, c, k):
                if not u.has_tile(c):
                    return
                v8 = (2 * u.j + c) % 8
                sub, h2 = v8 % 2, (v8 // 2) % 2
                mslot = 2 * (v8 // 4) + sub
                late = u.fixed is None or 2 * u.fixed + c >= 4
                if k == 0:
                    mask_wait(dve, u, c)
                if layer == 1:
                    dve.wait_ge(s["leaky"], u.at(2 * AK, AK * c + k + 1))
                else:
                    dve.wait_ge(s["scores"], u.at(2 * AK, AK * c + k + 1))
                if layer == 0 and late:
                    blocks = BLK // AK * (k + 1)
                    dve.wait_ge(s["turned"], u.at(BLK, BLK * ((c - 4) // 2) + blocks))
                dve.sem_inc(s["passed_dve"], 1)
                src = s_ps[:, k % 2, :] if layer == 0 else z[:, v8 % 4, k * AW:(k + 1) * AW]
                nc.vector.tensor_tensor_reduce(
                    out=z[:, v8 % 4, k * AW:(k + 1) * AW], in0=src, in1=mask[:, mslot, k * AW:(k + 1) * AW],
                    scale=1.0, scalar=LOWEST, op0=ALU.add, op1=ALU.max,
                    accum_out=mx[:, v8, k:k + 1]).then_inc(s["masked"], 1)

            def maximum(u, c):
                if not u.has_tile(c):
                    return
                v8 = (2 * u.j + c) % 8
                dve.wait_ge(s["masked"], u.at(2 * AK, AK * (c + 1)))
                nc.vector.tensor_reduce(nm[:, v8:v8 + 1], mx[:, v8, :], AX.X, ALU.max,
                                        negate=True).then_inc(s["max"], 1)

            def add_up(u):
                if not u.exists(-1):
                    return
                h2 = (u.j - 1) % 2
                v8 = (2 * u.j - 2) % 8
                parity = ((u.j - 1) % 4) // 2
                dve.wait_ge(s["exp"], u.at(8, 0))
                nc.vector.tensor_reduce(rsum[:, h2, :], rs[:, v8:v8 + 2, :], AX.X, ALU.add).then_inc(s["sums"], 1)
                dve.wait_ge(s["sums"], u.at(2, -1))
                nc.vector.reciprocal(rinv[:, h2, :], rsum[:, h2, :]).then_inc(s["sums"], 1)
                dve.wait_ge(s["sums"], u.at(2, 0))
                dve.wait_ge(res_in[parity], u.loop * 4 + 16 * ((u.j - 1) // 4 + 1))
                dve.wait_ge(s["o_turned"], u.at(1, 0))
                for sub in range(SUB):
                    r = res[:, parity, sub, DH * h2:DH * h2 + DH]
                    ins = nc.vector.scalar_tensor_tensor(
                        out=r, in0=o_ps[:, h2, 256 + DH * sub:256 + DH * sub + DH], scalar=rinv[:, h2, sub:sub + 1],
                        in1=r, op0=ALU.mult, op1=ALU.add)
                ins.then_inc(s["added"], 1)

            def body(u):
                for b in range(BLK):
                    copy_out(dve, u, b - 1, DVE_EVAC, "evac_dve")
                    if layer == 0:
                        masked(u, *((3, b) if b < 8 else (4, b - 8)))
                    elif b % 2:
                        leaky(u, *((3, b // 2) if b < 8 else (4, b // 2 - 4)))
                    else:
                        masked(u, *((2, 3) if b == 0 else (3, b // 2 - 1) if b < 9 else (4, b // 2 - 5)))
                    if b == layer:
                        maximum(u, 2)
                    if b == 8 + layer:
                        maximum(u, 3)
                    if b == 7:
                        add_up(u)
                    if layer == 0 and b == 3:
                        make_mask(u)

            if layer == 0:
                for sub in range(SUB):
                    convert(0, sub, sub, None)
            walk(dve, body)

        @block.scalar
        def _(act):
            def tile_chunk(n):
                return (1 + (n + 3) // 4, (n + 3) % 4)

            def exp(u, c, e):
                if not u.has_tile(c):
                    return
                v8 = (2 * u.j + c) % 8
                if e == 0:
                    act.wait_ge(s["max"], u.at(2, c + 1))
                    if u.fixed is None or 2 * u.fixed + c >= 8:
                        act.wait_ge(s["added"], u.at(1, c // 2 - 3))
                zc = z[:, v8 % 4, e * EW:(e + 1) * EW]
                nc.scalar.activation(zc, zc, ACT.Exp, bias=nm[:, v8:v8 + 1],
                                     accum_out=rs[:, v8, e:e + 1]).then_inc(s["exp"], 1)

            def copy_o(u):
                if not u.exists(-1):
                    return
                h2 = (u.j - 1) % 2
                act.wait_ge(s["pv"], u.at(BLK, 0))
                if u.exists(-3):
                    act.wait_ge(s["o_turned"], u.at(1, -2))
                nc.scalar.activation(o_sb[:, h2, :], o_ps[:, h2, 0:SUB * P], ACT.Copy).then_inc(s["o_copied"], 1)

            def body(u):
                for b in range(BLK):
                    copy_out(act, u, b - 1, ACT_EVAC, "evac_act")
                    if b == 3:
                        copy_o(u)
                    if b % 2 == layer:
                        exp(u, *tile_chunk(b // 2))

            walk(act, body)


def graph_layers(nc, x, adj, x2, v, w, a, out):
    with ExitStack() as ctx:
        count = [0]

        def sem(name):
            count[0] += 1
            return ctx.enter_context(nc.semaphore(name))

        ident = ctx.enter_context(nc.sbuf_tensor("ident", [P, P], F32))
        stack2 = ctx.enter_context(nc.sbuf_tensor("stack2", [P, DH], F32))
        f2 = ctx.enter_context(nc.sbuf_tensor("f2", [P, V_ALL], F32))
        ident_made = sem("ident_made")
        q_dram = nc.dram_tensor("q_parts", [PAIRS, NT, P, 2, P], F32, kind="Internal").ap()
        k_dram = nc.dram_tensor("k_parts", [H, P, N], F32, kind="Internal").ap()
        mask_dram = nc.dram_tensor("masks", [NT, P, N], BF16, kind="Internal").ap()
        x1_dram = nc.dram_tensor("x1", [N, D], F32, kind="Internal").ap()
        v1_dram = nc.dram_tensor("v1", [N, D], F32, kind="Internal").ap()
        f1_dram = nc.dram_tensor("f1", [2, H, N], F32, kind="Internal").ap()
        cleared = sem("ident_cleared")

        def make_ident(pool):
            nc.gpsimd.memset(ident[:], 0.0).then_inc(cleared, 1)
            nc.gpsimd.memset(stack2[:], 0.0).then_inc(cleared, 1)
            pool.wait_ge(cleared, 2)
            nc.gpsimd.affine_select(out=ident[:], in_=ident[:], compare_op=ALU.not_equal, fill=1.0, base=0,
                                    pattern=[[-1, P]], channel_multiplier=1).then_inc(ident_made, 1)
            nc.gpsimd.affine_select(out=stack2[:], in_=stack2[:], compare_op=ALU.not_equal, fill=1.0, base=0,
                                    pattern=[[-1, DH]], channel_multiplier=1).then_inc(cleared, 1)
            pool.wait_ge(cleared, 3)
            nc.gpsimd.affine_select(out=stack2[:], in_=stack2[:], compare_op=ALU.not_equal, fill=1.0, base=-DH,
                                    pattern=[[-1, DH]], channel_multiplier=1).then_inc(ident_made, 1)

        idp = (ident, ident_made)
        prepare0(nc, x, x2, q_dram, k_dram, idp, make_ident, sem)
        attend(nc, 0, x, x1_dram, v, mask_dram, idp, stack2, sem, adj=adj, q_dram=q_dram, k_dram=k_dram)
        prepare1(nc, x1_dram, w, a, v1_dram, f1_dram, f2, idp, sem)
        attend(nc, 1, x1_dram, out, v1_dram, mask_dram, idp, stack2, sem, f_dram=f1_dram, f2=f2)


def kernel(x, adj, L0_gnn_x2, L0_gnn_v, L1_gnn_W, L1_gnn_a):
    import numpy as np
    import concourse.bacc as bacc
    from concourse.bass_utils import run_bass_kernel_spmd

    nc = bacc.Bacc("TRN2", target_bir_lowering=False, num_devices=1)
    given = {"x": x, "adj": adj, "x2": L0_gnn_x2, "v": L0_gnn_v, "w": L1_gnn_W, "a": L1_gnn_a}
    arrays = {"in_" + n: np.ascontiguousarray(g) for n, g in given.items()}
    aps = [nc.dram_tensor(n, g.shape, mybir.dt.from_np(g.dtype), kind="ExternalInput").ap() for n, g in arrays.items()]
    out = nc.dram_tensor("out", [N, D], F32, kind="ExternalOutput").ap()
    graph_layers(nc, *aps, out)
    result = run_bass_kernel_spmd(nc, [arrays], core_ids=[0])
    return result.results[0]["out"]
```

```python
from contextlib import ExitStack

import concourse.bass as bass
from concourse import mybir
from concourse.alu_op_type import AluOpType as ALU

ACT = mybir.ActivationFunctionType
F32 = mybir.dt.float32
F32R = mybir.dt.float32r
BF16 = mybir.dt.bfloat16
I32 = mybir.dt.int32
AX = mybir.AxisListType

P = 128
N = 4096
D = 512
H = 8
DH = D // H
NT = N // P
PAIRS = H // 2
SUB = 2
GROUPS = NT // SUB
UNITS = H * GROUPS
V_ALL = UNITS * SUB
BLK = 16
CH = N // P
NEG = -float(2 ** 53)
LOWEST = -3.0e38
EPS = 1e-5
SCALE = DH ** -0.5
ALPHA = 0.2


class Unit:

    def __init__(self, loop, j, made=False, half=None):
        self.loop, self.j, self.made, self.half = loop, j, made, half
        self.fixed = loop + j if isinstance(loop, int) else None

    def at(self, a, b):
        if self.fixed is not None:
            return a * self.fixed + b
        return self.loop * a + (a * self.j + b)

    def exists(self, shift=0):
        return self.fixed is None or 0 <= self.fixed + shift < UNITS

    def has_tile(self, c):
        return self.fixed is None or 0 <= 2 * self.fixed + c < V_ALL

    def turns(self):
        return self.half + (self.j - self.j % 2) // 2 if self.fixed is None else self.fixed // 2

    @property
    def early(self):
        return self.fixed is not None and self.fixed < 2


def tiles(eng, *stages):
    most = max(lag for lag, _ in stages)

    def step(loop, j, half=None):
        for lag, stage in stages:
            if not isinstance(loop, int) or 0 <= loop + j - lag < NT:
                stage(Unit(loop, j - lag, half=half))

    for n in range(4):
        step(n - n % 2, n % 2)
    with eng.Fori(2, NT // 2) as i:
        for j in range(2):
            step(i * 2, j, i)
    for n in range(NT, NT + most):
        step(n - n % 2, n % 2)


def normalise(nc, eng, s, bufs):
    x_all, st, mean, work, rstd = bufs
    for c in range(4):
        eng.wait_ge(s["x_in"][c], 16)
        with eng.Fori(NT // 4 * c, NT // 4 * (c + 1)) as t:
            nc.vector.bn_stats(st[:, t, :], x_all[:, t, :]).then_inc(s["stats"], 1)
    eng.wait_ge(s["stats"], NT)
    n = [0]

    def link(ins):
        n[0] += 1
        ins.then_inc(s["norm"], 1)
        eng.wait_ge(s["norm"], n[0])

    me, ve, mo, vo = (st[:, :, i] for i in (1, 2, 4, 5))
    link(nc.vector.tensor_tensor(mean[:], me, mo, ALU.add))
    link(nc.vector.tensor_scalar(mean[:], mean[:], 0.5, None, ALU.mult))
    link(nc.vector.tensor_tensor(work[:, 0, :], me, mo, ALU.subtract))
    link(nc.vector.tensor_tensor(work[:, 1, :], work[:, 0, :], work[:, 0, :], ALU.mult))
    link(nc.vector.tensor_tensor(work[:, 2, :], ve, vo, ALU.add))
    link(nc.vector.tensor_scalar(work[:, 3, :], work[:, 2, :], 1.0 / D, EPS, ALU.mult, ALU.add))
    nc.vector.scalar_tensor_tensor(out=work[:, 4, :], in0=work[:, 1, :], scalar=0.25, in1=work[:, 3, :],
                                   op0=ALU.mult, op1=ALU.add).then_inc(s["var"], 1)
    eng.wait_ge(s["std"], 1)
    nc.vector.reciprocal(rstd[:], work[:, 5, :]).then_inc(s["rstd"], 1)
    eng.wait_ge(s["rstd"], 1)


def prepare0(nc, x, x2, q_dram, k_dram, ident, make_ident, sem):
    with ExitStack() as ctx:
        sb = lambda name, shape, dt: ctx.enter_context(nc.sbuf_tensor(name, shape, dt))
        x_all = sb("a_x_all", [P, NT, D], F32)
        st = sb("a_st", [P, NT, 6], F32)
        mean = sb("a_mean", [P, NT], F32)
        work = sb("a_work", [P, 6, NT], F32)
        rstd = sb("a_rstd", [P, NT], F32)
        xn = sb("a_xn", [P, 2, D], F32)
        hq = sb("a_hq", [P, 2, D], F32)
        kx = sb("a_kx", [P, 2, D], F32)
        q_st = sb("a_q_st", [P, 2, PAIRS, 2, P], F32R)
        k_st = sb("a_k_st", [P, 2, PAIRS, 2, P], F32R)
        tq = ctx.enter_context(nc.psum_tensor("a_tq", [P, 2, D], F32))
        tk = ctx.enter_context(nc.psum_tensor("a_tk", [P, 2, D], F32))
        s = {n: sem("a_" + n) for n in ("stats", "norm", "var", "std", "rstd", "xn", "h", "tq", "tk", "q_hi",
                                        "q_lo", "k_hi", "k_lo",
                                        "passed_pool")}
        s["x_in"] = [sem(f"a_x_in{c}") for c in range(4)]
        k_in = [sem(f"a_k_in{r}") for r in range(2)]
        q_out = [sem(f"a_q_out{r}") for r in range(2)]
        k_out = [[sem(f"a_k_out{r}{e}") for e in range(2)] for r in range(2)]
        x_t = x.rearrange("(t p) d -> p t d", p=P)
        x2_t = x2.rearrange("(t p) d -> t p d", p=P)
        block = ctx.enter_context(nc.Block())

        def store_keys(eng, t, e):
            r = t.j % 2
            for h2 in range(2):
                dst = k_dram.rearrange("(a h) (b d) (t m) -> h b t d a m", h=2, b=2, m=P)[h2, e, t.at(1, 0)]
                eng.dma_start(dst, k_st[DH * h2:DH * h2 + DH, r, :, e, :].bitcast(F32)).then_inc(k_out[r][e], 16)

        @block.sync
        def _(sp):
            for c in range(4):
                sp.dma_start(x_all[:, 8 * c:8 * c + 8, :], x_t[:, 8 * c:8 * c + 8, :]).then_inc(s["x_in"][c], 16)

            def load(t):
                r = t.j % 2
                if not t.early:
                    sp.wait_ge(s["tk"], t.at(1, -1))
                sp.dma_start(kx[:, r, :], x2_t[t.at(1, 0)]).then_inc(k_in[r], 16)

            def store(t):
                r = t.j % 2
                sp.wait_ge(s["k_lo"], t.at(1, 1))
                store_keys(sp, t, 1)
                sp.wait_ge(s["q_lo"], t.at(1, 1))
                sp.dma_start(q_dram[:, t.at(1, 0), :, :, :].rearrange("a p b n -> p a b n"),
                             q_st[:, r].bitcast(F32)).then_inc(q_out[r], 16)

            tiles(sp, (0, load), (2, store))
            for r in range(2):
                sp.wait_ge(q_out[r], 16 * (NT // 2))
                for e in range(2):
                    sp.wait_ge(k_out[r][e], 32 * (NT // 2))

        @block.gpsimd
        def _(pool):
            make_ident(pool)

            def store(t):
                pool.wait_ge(s["k_hi"], t.at(1, 1))
                pool.sem_inc(s["passed_pool"], 1)
                store_keys(pool, t, 0)

            tiles(pool, (0, store))

        @block.vector
        def _(dve):
            normalise(nc, dve, s, (x_all, st, mean, work, rstd))

            def norm(t):
                r = t.j % 2
                if not t.early:
                    dve.wait_ge(s["h"], t.at(1, -1))
                nc.vector.tensor_scalar(xn[:, r, :], x_all[:, t.at(1, 0), :], mean[:, bass.ds(t.at(1, 0), 1)],
                                        rstd[:, bass.ds(t.at(1, 0), 1)], ALU.subtract, ALU.mult).then_inc(s["xn"], 1)

            def low(t):
                r = t.j % 2
                for ps, staged, n in ((tk, k_st, "k"), (tq, q_st, "q")):
                    dve.wait_ge(s[n + "_hi"], t.at(1, 1))
                    nc.vector.tensor_tensor(staged[:, r, :, 1, :], ps[:, r].rearrange("p (a n) -> p a n", n=P),
                                            staged[:, r, :, 0, :], ALU.subtract).then_inc(s[n + "_lo"], 1)

            tiles(dve, (0, norm), (1, low))

        @block.scalar
        def _(act):
            act.wait_ge(s["var"], 1)
            nc.scalar.activation(work[:, 5, :], work[:, 4, :], ACT.Sqrt).then_inc(s["std"], 1)

            def relu(t):
                r = t.j % 2
                act.wait_ge(s["xn"], t.at(1, 1))
                if not t.early:
                    act.wait_ge(s["tq"], t.at(1, -1))
                nc.scalar.activation(hq[:, r, :], xn[:, r, :], ACT.Relu, scale=SCALE).then_inc(s["h"], 1)

            def high(t):
                r = t.j % 2
                for ps, staged, outs, per, n in ((tk, k_st, k_out[r], 32, "k"), (tq, q_st, (q_out[r],), 16, "q")):
                    act.wait_ge(s["t" + n], t.at(1, 1))
                    if not t.early:
                        for out in outs:
                            act.wait_ge(out, t.turns() * per)
                    nc.scalar.activation(staged[:, r, :, 0, :], ps[:, r].rearrange("p (a n) -> p a n", n=P),
                                         ACT.Copy).then_inc(s[n + "_hi"], 1)

            tiles(act, (0, relu), (1, high))

        @block.tensor
        def _(pe):
            pe.wait_ge(ident[1], 2)

            def turn(t):
                r = t.j % 2
                pe.wait_ge(k_in[r], t.turns() * 16 + 16)
                if not t.early:
                    pe.wait_ge(s["k_lo"], t.at(1, -1))
                for a in range(PAIRS):
                    mm = pe.transpose(tk[:, r, a * P:(a + 1) * P], kx[:, r, a * P:(a + 1) * P], ident[0][:])
                mm.then_inc(s["tk"], 1)
                pe.wait_ge(s["h"], t.at(1, 1))
                if not t.early:
                    pe.wait_ge(s["q_lo"], t.at(1, -1))
                for a in range(PAIRS):
                    mm = pe.transpose(tq[:, r, a * P:(a + 1) * P], hq[:, r, a * P:(a + 1) * P], ident[0][:])
                mm.then_inc(s["tq"], 1)

            tiles(pe, (0, turn))


def prepare1(nc, x1, w, a, v_dram, f_dram, f2, ident, sem):
    with ExitStack() as ctx:
        sb = lambda name, shape, dt: ctx.enter_context(nc.sbuf_tensor(name, shape, dt))
        x_all = sb("c_x_all", [P, NT, D], F32)
        st = sb("c_st", [P, NT, 6], F32)
        mean = sb("c_mean", [P, NT], F32)
        work = sb("c_work", [P, 6, NT], F32)
        rstd = sb("c_rstd", [P, NT], F32)
        w_sb = sb("c_w", [P, D // P, D], F32)
        a_bc = sb("c_a_bc", [P, 2, D], F32)
        xn = sb("c_xn", [P, 2, D], F32)
        hn = sb("c_hn", [P, 2, D], F32)
        ht = sb("c_ht", [P, 2, D], F32)
        hw_sb = sb("c_hw_sb", [P, 2, D], F32)
        prod = sb("c_prod", [P, 2, 2, D], F32)
        f1 = sb("c_f1", [P, H, NT], F32)
        f_rows = sb("c_f_rows", [P, 2, 2, P], F32)
        th = ctx.enter_context(nc.psum_tensor("c_th", [P, 2, D], F32))
        hw = ctx.enter_context(nc.psum_tensor("c_hw", [P, 2, D], F32))
        tf = ctx.enter_context(nc.psum_tensor("c_tf", [P, 2, P], F32))
        s = {n: sem("c_" + n) for n in ("stats", "norm", "var", "std", "rstd", "xn", "h", "th", "ht", "hw", "hw_sb",
                                        "prod", "f", "w_in", "a_in", "tf", "f_rows", "f_out", "f2")}
        s["x_in"] = [sem(f"c_x_in{c}") for c in range(4)]
        v_out = [sem(f"c_v_out{r}") for r in range(2)]
        x_t = x1.rearrange("(t p) d -> p t d", p=P)
        v_t = v_dram.rearrange("(t p) d -> t p d", p=P)
        block = ctx.enter_context(nc.Block())

        @block.sync
        def _(sp):
            for c in range(4):
                sp.dma_start(x_all[:, 8 * c:8 * c + 8, :], x_t[:, 8 * c:8 * c + 8, :]).then_inc(s["x_in"][c], 16)
            for c in range(D // P):
                sp.dma_start(w_sb[:, c, :].rearrange("p (k q) -> p k q", k=H),
                             w[:, c * P:(c + 1) * P, :].rearrange("k f q -> f k q")).then_inc(s["w_in"], 16)
            for e in range(2):
                src = a[:, e * DH:(e + 1) * DH, 0].unsqueeze(0).to_broadcast([P, H, DH])
                sp.dma_start(a_bc[:, e, :].rearrange("p (k q) -> p k q", k=H), src).then_inc(s["a_in"], 16)

            def store(t):
                r = t.j % 2
                sp.wait_ge(s["hw_sb"], t.at(1, 1))
                sp.dma_start(v_t[t.at(1, 0)], hw_sb[:, r, :]).then_inc(v_out[r], 16)

            tiles(sp, (2, store))
            sp.wait_ge(s["f_rows"], 2)
            for e in range(2):
                sp.dma_start(f_dram[e].rearrange("k (t n) -> (k t) n", n=P).rearrange("(j p) n -> p j n", p=P),
                             f_rows[:, e]).then_inc(s["f_out"], 16)
            sp.wait_ge(s["f_out"], 32)
            for r in range(2):
                sp.wait_ge(v_out[r], 16 * (NT // 2))

        @block.vector
        def _(dve):
            normalise(nc, dve, s, (x_all, st, mean, work, rstd))
            dve.wait_ge(s["a_in"], 32)

            def norm(t):
                r = t.j % 2
                if not t.early:
                    dve.wait_ge(s["h"], t.at(1, -1))
                nc.vector.tensor_scalar(xn[:, r, :], x_all[:, t.at(1, 0), :], mean[:, bass.ds(t.at(1, 0), 1)],
                                        rstd[:, bass.ds(t.at(1, 0), 1)], ALU.subtract, ALU.mult).then_inc(s["xn"], 1)

            def dots(t):
                r = t.j % 2
                dve.wait_ge(s["hw_sb"], t.at(1, 1))
                if not t.early:
                    dve.wait_ge(s["f"], t.at(2, -2))
                for e in range(2):
                    nc.vector.tensor_tensor(prod[:, r, e, :], hw_sb[:, r, :], a_bc[:, e, :],
                                            ALU.mult).then_inc(s["prod"], 1)
                f2_v = f2[:].rearrange("p (a g h s) -> p a h g s", a=PAIRS, h=2, s=SUB)
                g = t.turns()
                for e, dst in enumerate((f1[:, :, t.at(1, 0)], f2_v[:, :, :, g, r])):
                    dve.wait_ge(s["prod"], t.at(2, e + 1))
                    src = prod[:, r, e, :]
                    src = (src.rearrange("p (k q) -> p k q", k=H) if e == 0 else
                           src.rearrange("p (a h q) -> p a h q", a=PAIRS, h=2))
                    nc.vector.tensor_reduce(dst, src, AX.X, ALU.add).then_inc(s["f"], 1)

            tiles(dve, (0, norm), (3, dots))
            dve.wait_ge(s["tf"], 1)
            nc.vector.tensor_copy(f_rows[:, 0], tf[:]).then_inc(s["f_rows"], 1)
            nc.vector.tensor_scalar(f_rows[:, 1], tf[:], ALPHA, None, ALU.mult).then_inc(s["f_rows"], 1)
            dve.wait_ge(s["f"], 2 * NT)
            nc.vector.tensor_scalar(f2[:], f2[:], 1.0 - ALPHA, None, ALU.mult).then_inc(s["f2"], 1)
            dve.wait_ge(s["f2"], 1)

        @block.scalar
        def _(act):
            act.wait_ge(s["var"], 1)
            nc.scalar.activation(work[:, 5, :], work[:, 4, :], ACT.Sqrt).then_inc(s["std"], 1)

            def relu(t):
                r = t.j % 2
                act.wait_ge(s["xn"], t.at(1, 1))
                if not t.early:
                    act.wait_ge(s["th"], t.at(1, -1))
                nc.scalar.activation(hn[:, r, :], xn[:, r, :], ACT.Relu).then_inc(s["h"], 1)

            def copy_h(t):
                r = t.j % 2
                act.wait_ge(s["th"], t.at(1, 1))
                if not t.early:
                    act.wait_ge(s["hw"], t.at(1, -1))
                nc.scalar.activation(ht[:, r, :], th[:, r, :], ACT.Copy).then_inc(s["ht"], 1)

            def copy_hw(t):
                r = t.j % 2
                act.wait_ge(s["hw"], t.at(1, 1))
                if not t.early:
                    act.wait_ge(v_out[r], t.turns() * 16)
                    act.wait_ge(s["prod"], t.at(2, -2))
                nc.scalar.activation(hw_sb[:, r, :], hw[:, r, :], ACT.Copy).then_inc(s["hw_sb"], 1)

            tiles(act, (0, relu), (2, copy_hw), (1, copy_h))

        @block.tensor
        def _(pe):
            pe.wait_ge(s["w_in"], 16 * (D // P))

            def turn(t):
                r = t.j % 2
                pe.wait_ge(s["h"], t.at(1, 1))
                if not t.early:
                    pe.wait_ge(s["ht"], t.at(1, -1))
                for c in range(D // P):
                    mm = pe.transpose(th[:, r, c * P:(c + 1) * P], hn[:, r, c * P:(c + 1) * P], ident[0][:])
                mm.then_inc(s["th"], 1)

            def product(t):
                r = t.j % 2
                pe.wait_ge(s["ht"], t.at(1, 1))
                if not t.early:
                    pe.wait_ge(s["hw_sb"], t.at(1, -1))
                for c in range(D // P):
                    mm = pe.matmul(hw[:, r, :], ht[:, r, c * P:(c + 1) * P], w_sb[:, c, :],
                                   start=(c == 0), stop=(c == D // P - 1))
                mm.then_inc(s["hw"], 1)

            tiles(pe, (0, turn), (1, product))
            pe.wait_ge(s["f"], 2 * NT)
            for j in range(2):
                mm = pe.transpose(tf[:, j, :], f1[:].rearrange("p k t -> p (k t)")[:, j * P:(j + 1) * P], ident[0][:])
            mm.then_inc(s["tf"], 1)


def attend(nc, layer, x_in, x_out, v_dram, mask_dram, ident, stack2, sem, adj=None, q_dram=None, k_dram=None,
           f_dram=None, f2=None):
    name = "bd"[layer] + "_"
    AK = 8 if layer == 0 else 2
    AW = N // AK
    EK, EW = 4, N // 4
    ACT_EVAC = [b for b in range(BLK) if (b % 2 or layer == 1)]
    DVE_EVAC = [b for b in range(BLK) if b not in ACT_EVAC]
    with ExitStack() as ctx:
        sb = lambda n, shape, dt: ctx.enter_context(nc.sbuf_tensor(name + n, shape, dt))
        z = sb("z", [P, 4, N], F32)
        mask = sb("mask", [P, 4, N], BF16)
        v_sb = sb("v", [P, 2, CH, DH], F32)
        pt = sb("pt", [P, 4, 512], F32)
        o_sb = sb("o_sb", [P, 2, 2 * P], F32)
        res = sb("res", [P, 2, SUB, P], F32)
        mx = sb("mx", [P, 8, AK], F32)
        nm = sb("nm", [P, 8], F32)
        rs = sb("rs", [P, 8, EK], F32)
        rsum = sb("rsum", [P, 2, 2], F32)
        rinv = sb("rinv", [P, 2, 2], F32)
        if layer == 0:
            k_sb = sb("k", [P, 2, N], F32R)
            q_sb = sb("q", [P, 4, 2, P], F32R)
            adj_sb = sb("adj", [P, 2, N], I32)
        else:
            f_bc = sb("f_bc", [P, 2, 2, N], F32)
        t_ps = ctx.enter_context(nc.psum_tensor(name + "t_ps", [P, 4, 512], F32))
        o_ps = ctx.enter_context(nc.psum_tensor(name + "o_ps", [P, 2, 512], F32))
        s_ps = ctx.enter_context(nc.psum_tensor(name + "s_ps", [P, 2, 512], F32))

        s = {n: sem(name + n) for n in (
            "scores", "masked", "max", "exp", "leaky", "turned", "evac_act", "evac_dve", "pv", "o_copied", "o_turned",
            "added", "conv", "sums", "link", "passed_dve", "passed_act", "passed_pool")}
        mask_in = [sem(f"{name}mask_in{i}") for i in range(4)]
        mask_out = [sem(f"{name}mask_out{i}") for i in range(4)]
        q_in = [sem(f"{name}q_in{i}") for i in range(4)]
        key_in = [sem(f"{name}key_in{i}") for i in range(2)]
        v_in = [sem(f"{name}v_in{i}") for i in range(2)]
        adj_in = [sem(f"{name}adj_in{i}") for i in range(2)]
        res_in = [sem(f"{name}res_in{i}") for i in range(2)]
        res_out = [sem(f"{name}res_out{i}") for i in range(2)]
        x_g = x_in.rearrange("(g s p) d -> g p s d", s=SUB, p=P)
        y_g = x_out.rearrange("(g s p) d -> g p s d", s=SUB, p=P)
        v_c = v_dram.rearrange("(c p) d -> p c d", p=P)
        LAST = UNITS // 4 - 1
        if layer == 0:
            segments = [("static", -2, 4), ("loop", 1, 7), ("static", 28, 32), ("loop", 8, LAST),
                        ("static", 4 * LAST, UNITS + 1)]
        else:
            segments = [("static", -2, 4), ("loop", 1, LAST), ("static", 4 * LAST, UNITS + 1)]
        UP = 2 * GROUPS

        def f2_of(u, c):
            return f2[:, bass.ds(u.loop * 2 + (2 * u.j + c), 1)]

        def evac_wait(eng, u, b):
            du, b = divmod(b, BLK)
            if not u.exists(du):
                return
            which, own = ("evac_act", ACT_EVAC) if b in ACT_EVAC else ("evac_dve", DVE_EVAC)
            eng.wait_ge(s[which], u.at(len(own), len(own) * du + own.index(b) + 1))

        def walk(eng, body):
            for kind, a, b in segments:
                if kind == "static":
                    for n in range(a, b):
                        body(Unit(4 * (n // 4), n % 4))
                else:
                    with eng.Fori(a, b) as i:
                        for j in range(4):
                            body(Unit(i * 4, j, made=layer == 0 and a == 1))

        block = ctx.enter_context(nc.Block())

        @block.sync
        def _(sp):
            def load_keys(p, h2):
                if p:
                    last = 4 * GROUPS * p - (3 if h2 == 0 else 1)
                    if layer == 0:
                        sp.wait_ge(s["scores"], AK * (last + 1))
                    else:
                        sp.wait_ge(s["leaky"], AK * (last + 1))
                if layer == 0:
                    sp.dma_start(k_sb[:, h2, :].bitcast(F32), k_dram[2 * p + h2]).then_inc(key_in[h2], 16)
                else:
                    for e in range(2):
                        sp.dma_start(f_bc[:, h2, e, :], f_dram[e, 2 * p + h2:2 * p + h2 + 1, :].to_broadcast([P, N]))\
                            .then_inc(key_in[h2], 16)

            def load_values(p, h2):
                if p:
                    sp.wait_ge(s["pv"], BLK * (UP * p - 1 + h2))
                col = (2 * p + h2) * DH
                sp.dma_start(v_sb[:, h2], v_c[:, :, col:col + DH]).then_inc(v_in[h2], 16)

            def load_queries(p, g, first=False, heads=(0, 1)):
                for i in range(2 * heads[0], 2 * heads[-1] + 2):
                    h2, sub = divmod(i, 2)
                    if not first:
                        sp.wait_ge(s["scores"], g * (4 * AK) + AK * (4 * GROUPS * p + i - 3))
                    src = q_dram[p, g * SUB + sub, DH * h2:DH * h2 + DH].rearrange("d b n -> d (b n)")
                    for half in range(2):
                        sp.dma_start(q_sb[DH * half:DH * half + DH, i].rearrange("d b n -> d (b n)").bitcast(F32),
                                     src).then_inc(q_in[i], 16)

            def load_masks(slot2, g, wait):
                for sub in range(SUB):
                    if wait is not None:
                        sp.wait_ge(s["masked"], wait)
                    sp.dma_start(mask[:, 2 * slot2 + sub, :], mask_dram[g * SUB + sub])\
                        .then_inc(mask_in[2 * slot2 + sub], 16)

            def load_adj(t, sub, first=False):
                if not first:
                    sp.wait_ge(s["conv"], t + (-1))
                sp.dma_start(adj_sb[:, sub, :], adj.rearrange("(t p) m -> t p m", p=P)[t]).then_inc(adj_in[sub], 16)

            def store_rows(p, g, parity):
                sp.wait_ge(s["added"], g * 2 + (UP * p + 2))
                sp.dma_start(y_g[g][:, :, P * p:P * p + P], res[:, parity]).then_inc(res_out[parity], 16)

            def load_rows(p, g, parity, first):
                if not first:
                    sp.wait_ge(res_out[parity], (g - parity) * 8 + 8 * GROUPS * p)
                sp.dma_start(res[:, parity], x_g[g][:, :, P * p:P * p + P]).then_inc(res_in[parity], 16)

            if layer == 0:
                load_adj(0, 0, True)
                load_adj(1, 1, True)
                load_queries(0, 0, True)
                load_keys(0, 0)
                load_keys(0, 1)
                load_values(0, 0)
                load_values(0, 1)
            else:
                load_keys(0, 0)
                load_masks(0, 0, None)
                load_keys(0, 1)
                load_values(0, 0)
                load_values(0, 1)
                load_masks(1, 1, None)

            def step(p, g, parity, edge=None):
                made = layer == 0 and p == 0
                last = edge == GROUPS - 1
                if last and p + 1 == PAIRS:
                    pass
                elif last:
                    for i in range(4 if made else 0):
                        sp.wait_ge(mask_out[i], 16 * (GROUPS // 2))
                    load_masks(0, 0, 4 * AK * (GROUPS * (p + 1) - 1))
                elif made:
                    for sub in range(SUB):
                        load_adj(g * 2 + (2 + sub), sub)
                elif not (edge == 0 and p == 0):
                    load_masks(1 - parity, g + 1, g * (4 * AK) + 4 * AK * (GROUPS * p))
                if edge == 0 and p:
                    load_values(p, 0)
                    load_values(p, 1)
                if last and p + 1 < PAIRS:
                    load_keys(p + 1, 0)
                    if layer == 0:
                        load_queries(p + 1, 0, heads=(0,))
                    load_keys(p + 1, 1)
                if edge in (0, 1) and p:
                    store_rows(p - 1, GROUPS - 2 + edge, parity)
                elif edge not in (0, 1):
                    store_rows(p, g - 2, parity)
                load_rows(p, g, parity, first=edge in (0, 1) and p == 0)
                if layer == 0 and not last:
                    load_queries(p, g + 1)
                elif layer == 0 and p + 1 < PAIRS:
                    load_queries(p + 1, 0, heads=(1,))

            for p in range(PAIRS):
                for g in (0, 1):
                    step(p, g, g, edge=g)
                with sp.Fori(1, GROUPS // 2 - 1) as i:
                    for parity in range(2):
                        step(p, i * 2 + parity, parity)
                for g in (GROUPS - 2, GROUPS - 1):
                    step(p, g, g % 2, edge=g)
            for g in (GROUPS - 2, GROUPS - 1):
                store_rows(PAIRS - 1, g, g % 2)
            for parity in range(2):
                sp.wait_ge(res_out[parity], 8 * GROUPS * PAIRS)

        @block.gpsimd
        def _(pool):
            def keep_masks(g, parity):
                for sub in range(SUB):
                    pool.wait_ge(s["conv"], g * 2 + (sub + 1))
                    pool.sem_inc(s["passed_pool"], 1)
                    pool.dma_start(mask_dram[g * SUB + sub], mask[:, 2 * parity + sub, :])\
                        .then_inc(mask_out[2 * parity + sub], 16)

            if layer == 0:
                with pool.Fori(0, GROUPS // 2) as i:
                    for parity in range(2):
                        keep_masks(i * 2 + parity, parity)

        def mask_wait(eng, u, c):
            w = 2 * u.j + c
            slot = 2 * (w % 8 // 4) + w % 2
            if layer == 0 and (u.made if u.fixed is None else 2 * u.fixed + c < 4 * GROUPS):
                eng.wait_ge(s["conv"], u.loop + (2 * (w // 4) + w % 2 + 1))
            else:
                skip = GROUPS // 2 if layer == 0 else 0
                eng.wait_ge(mask_in[slot], u.loop * 4 + 16 * (w // 8 + 1 - skip))

        @block.tensor
        def _(pe):
            def body(u):
                for b in range(BLK):
                    if u.exists():
                        if b % 4 == 0:
                            pe.wait_ge(s["exp"], u.at(8, 5 + b // 4))
                        evac_wait(pe, u, b - 4)
                        for i in range(2):
                            for sub in range(SUB):
                                c = 2 * b + i
                                mm = pe.transpose(t_ps[:, b % 4, (2 * i + sub) * P:(2 * i + sub + 1) * P],
                                                  z[:, 2 * (u.j % 2) + sub, c * P:(c + 1) * P], ident[0][:])
                        mm.then_inc(s["turned"], 1)
                    if layer == 0:
                        c, k = (3, b) if b < 8 else (4, b - 8)
                        if u.has_tile(c):
                            v4 = (2 * u.j + c) % 4
                            h2 = v4 // 2
                            if k == 0:
                                pe.wait_ge(q_in[v4], u.loop * 16 + 32 * ((2 * u.j + c) // 4 + 1))
                                pe.wait_ge(key_in[h2], (u.at(1, c // 2) // UP) * 16 + 16)
                            if not (u.fixed is not None and 2 * u.fixed + c == 0 and k < 2):
                                pe.wait_ge(s["masked"], u.at(2 * AK, AK * c + k - 1))
                            for e in range(2):
                                mm = pe.matmul(s_ps[:, k % 2, :], q_sb[:, v4, e, :],
                                               k_sb[:, h2, k * AW:(k + 1) * AW], start=(e == 0), stop=(e == 1))
                            mm.then_inc(s["scores"], 1)
                    du, b2 = divmod(b - 3, BLK)
                    if u.exists(du):
                        h2 = (u.j + du) % 2
                        if b2 == 0:
                            pe.wait_ge(v_in[h2], (u.at(1, du) // UP) * 16 + 16)
                            if u.exists(du - 2):
                                pe.wait_ge(s["added"], u.at(1, du - 1))
                        evac_wait(pe, u, b - 3)
                        for i in range(2):
                            mm = pe.matmul(o_ps[DH * i:DH * i + DH, h2, 0:SUB * P], v_sb[:, h2, 2 * b2 + i, :],
                                           pt[:, b2 % 4, i * 256:(i + 1) * 256], start=(b2 == 0),
                                           stop=(b2 == BLK - 1))
                        mm.then_inc(s["pv"], 1)
                    if b == 5 and u.exists(-1):
                        h2 = (u.j - 1) % 2
                        pe.wait_ge(s["o_copied"], u.at(1, 0))
                        for sub in range(SUB):
                            mm = pe.matmul(o_ps[:, h2, 256 + DH * sub:256 + DH * sub + DH],
                                           o_sb[:, h2, sub * P:(sub + 1) * P], stack2[:], start=True, stop=True,
                                           skip_group_check=True)
                        mm.then_inc(s["o_turned"], 1)

            walk(pe, body)

        def copy_out(eng, u, b, own, done):
            du, b = divmod(b, BLK)
            if b not in own or not u.exists(du):
                return
            eng.wait_ge(s["turned"], u.at(BLK, BLK * du + b + 1))
            if not (u.fixed is not None and BLK * (u.fixed + du) + b < 4):
                eng.wait_ge(s["pv"], u.at(BLK, BLK * du + b - 3))
            if done == "evac_act":
                nc.scalar.activation(pt[:, b % 4, :], t_ps[:, b % 4, :], ACT.Copy).then_inc(s[done], 1)
            else:
                nc.vector.tensor_copy(pt[:, b % 4, :], t_ps[:, b % 4, :]).then_inc(s[done], 1)

        @block.vector
        def _(dve):
            def convert(tile, slot, sub, reuse):
                dve.wait_ge(adj_in[sub], tile_in(tile))
                if reuse is not None:
                    dve.wait_ge(mask_out[slot], reuse)
                nc.vector.tensor_scalar(mask[:, slot, :], adj_sb[:, sub, :], 0, NEG, ALU.is_le,
                                        ALU.mult).then_inc(s["conv"], 1)

            def tile_in(tile):
                return tile * 16 + 16

            def make_mask(u):
                sub = 0 if u.j % 2 else 1
                if u.fixed is not None:
                    g = (u.fixed + 3 - sub) // 2
                    if u.fixed < -2 or g >= GROUPS or (u.fixed == -2):
                        return
                    convert(g, 2 * (g % 2) + sub, sub, 16 * (g // 2) if g >= 2 else None)
                elif u.made:
                    dg = (u.j + 3 - sub) // 2
                    slot = 2 * (dg % 2) + sub
                    dve.wait_ge(adj_in[sub], u.loop * 8 + (16 * dg + 16))
                    dve.wait_ge(mask_out[slot], u.loop * 4 + 16 * (dg // 2))
                    nc.vector.tensor_scalar(mask[:, slot, :], adj_sb[:, sub, :], 0, NEG, ALU.is_le,
                                            ALU.mult).then_inc(s["conv"], 1)

            def leaky(u, c, k):
                if not u.has_tile(c):
                    return
                v8 = (2 * u.j + c) % 8
                h2 = (v8 // 2) % 2
                if k == 0:
                    dve.wait_ge(key_in[h2], (u.at(1, c // 2) // UP) * 32 + 32)
                if u.fixed is None or 2 * u.fixed + c >= 4:
                    dve.wait_ge(s["turned"], u.at(BLK, BLK * ((c - 4) // 2) + BLK // AK * (k + 1)))
                dve.sem_inc(s["passed_dve"], 1)
                cols = slice(k * AW, (k + 1) * AW)
                nc.vector.scalar_tensor_tensor(out=z[:, v8 % 4, cols], in0=f_bc[:, h2, 0, cols], scalar=f2_of(u, c),
                                               in1=f_bc[:, h2, 1, cols], op0=ALU.add,
                                               op1=ALU.max).then_inc(s["leaky"], 1)

            def masked(u, c, k):
                if not u.has_tile(c):
                    return
                v8 = (2 * u.j + c) % 8
                sub, h2 = v8 % 2, (v8 // 2) % 2
                mslot = 2 * (v8 // 4) + sub
                late = u.fixed is None or 2 * u.fixed + c >= 4
                if k == 0:
                    mask_wait(dve, u, c)
                if layer == 1:
                    dve.wait_ge(s["leaky"], u.at(2 * AK, AK * c + k + 1))
                else:
                    dve.wait_ge(s["scores"], u.at(2 * AK, AK * c + k + 1))
                if layer == 0 and late:
                    blocks = BLK // AK * (k + 1)
                    dve.wait_ge(s["turned"], u.at(BLK, BLK * ((c - 4) // 2) + blocks))
                dve.sem_inc(s["passed_dve"], 1)
                src = s_ps[:, k % 2, :] if layer == 0 else z[:, v8 % 4, k * AW:(k + 1) * AW]
                nc.vector.tensor_tensor_reduce(
                    out=z[:, v8 % 4, k * AW:(k + 1) * AW], in0=src, in1=mask[:, mslot, k * AW:(k + 1) * AW],
                    scale=1.0, scalar=LOWEST, op0=ALU.add, op1=ALU.max,
                    accum_out=mx[:, v8, k:k + 1]).then_inc(s["masked"], 1)

            def maximum(u, c):
                if not u.has_tile(c):
                    return
                v8 = (2 * u.j + c) % 8
                dve.wait_ge(s["masked"], u.at(2 * AK, AK * (c + 1)))
                nc.vector.tensor_reduce(nm[:, v8:v8 + 1], mx[:, v8, :], AX.X, ALU.max,
                                        negate=True).then_inc(s["max"], 1)

            def add_up(u):
                if not u.exists(-1):
                    return
                h2 = (u.j - 1) % 2
                v8 = (2 * u.j - 2) % 8
                parity = ((u.j - 1) % 4) // 2
                dve.wait_ge(s["exp"], u.at(8, 0))
                nc.vector.tensor_reduce(rsum[:, h2, :], rs[:, v8:v8 + 2, :], AX.X, ALU.add).then_inc(s["sums"], 1)
                dve.wait_ge(s["sums"], u.at(2, -1))
                nc.vector.reciprocal(rinv[:, h2, :], rsum[:, h2, :]).then_inc(s["sums"], 1)
                dve.wait_ge(s["sums"], u.at(2, 0))
                dve.wait_ge(res_in[parity], u.loop * 4 + 16 * ((u.j - 1) // 4 + 1))
                dve.wait_ge(s["o_turned"], u.at(1, 0))
                for sub in range(SUB):
                    r = res[:, parity, sub, DH * h2:DH * h2 + DH]
                    ins = nc.vector.scalar_tensor_tensor(
                        out=r, in0=o_ps[:, h2, 256 + DH * sub:256 + DH * sub + DH], scalar=rinv[:, h2, sub:sub + 1],
                        in1=r, op0=ALU.mult, op1=ALU.add)
                ins.then_inc(s["added"], 1)

            def body(u):
                for b in range(BLK):
                    copy_out(dve, u, b - 1, DVE_EVAC, "evac_dve")
                    if layer == 0:
                        masked(u, *((3, b) if b < 8 else (4, b - 8)))
                    elif b % 4 == 1:
                        leaky(u, 3 + b // 8, b // 4 % 2)
                    elif b % 4 == 3:
                        masked(u, 2 + (b // 4 + 1) // 2, (b // 4 + 1) % 2)
                    if b == 4 * layer:
                        maximum(u, 2)
                    if b == 8 + 4 * layer:
                        maximum(u, 3)
                    if b == 7:
                        add_up(u)
                    if layer == 0 and b == 3:
                        make_mask(u)

            if layer == 0:
                for sub in range(SUB):
                    convert(0, sub, sub, None)
            walk(dve, body)

        @block.scalar
        def _(act):
            def tile_chunk(n):
                n += 3 - layer
                return (1 + n // 4, n % 4)

            def exp(u, c, e):
                if not u.has_tile(c):
                    return
                v8 = (2 * u.j + c) % 8
                if e == 0:
                    act.wait_ge(s["max"], u.at(2, c + 1))
                    if u.fixed is None or 2 * u.fixed + c >= 8:
                        act.wait_ge(s["added"], u.at(1, c // 2 - 3))
                zc = z[:, v8 % 4, e * EW:(e + 1) * EW]
                nc.scalar.activation(zc, zc, ACT.Exp, bias=nm[:, v8:v8 + 1],
                                     accum_out=rs[:, v8, e:e + 1]).then_inc(s["exp"], 1)

            def copy_o(u):
                if not u.exists(-1):
                    return
                h2 = (u.j - 1) % 2
                act.wait_ge(s["pv"], u.at(BLK, 0))
                if u.exists(-3):
                    act.wait_ge(s["o_turned"], u.at(1, -2))
                nc.scalar.activation(o_sb[:, h2, :], o_ps[:, h2, 0:SUB * P], ACT.Copy).then_inc(s["o_copied"], 1)

            def body(u):
                for b in range(BLK):
                    copy_out(act, u, b - 1, ACT_EVAC, "evac_act")
                    if b == 3:
                        copy_o(u)
                    if b % 2 == layer:
                        exp(u, *tile_chunk(b // 2))

            walk(act, body)


def graph_layers(nc, x, adj, x2, v, w, a, out):
    with ExitStack() as ctx:
        count = [0]

        def sem(name):
            count[0] += 1
            return ctx.enter_context(nc.semaphore(name))

        ident = ctx.enter_context(nc.sbuf_tensor("ident", [P, P], F32))
        stack2 = ctx.enter_context(nc.sbuf_tensor("stack2", [P, DH], F32))
        f2 = ctx.enter_context(nc.sbuf_tensor("f2", [P, V_ALL], F32))
        ident_made = sem("ident_made")
        q_dram = nc.dram_tensor("q_parts", [PAIRS, NT, P, 2, P], F32, kind="Internal").ap()
        k_dram = nc.dram_tensor("k_parts", [H, P, N], F32, kind="Internal").ap()
        mask_dram = nc.dram_tensor("masks", [NT, P, N], BF16, kind="Internal").ap()
        x1_dram = nc.dram_tensor("x1", [N, D], F32, kind="Internal").ap()
        v1_dram = nc.dram_tensor("v1", [N, D], F32, kind="Internal").ap()
        f1_dram = nc.dram_tensor("f1", [2, H, N], F32, kind="Internal").ap()
        cleared = sem("ident_cleared")

        def make_ident(pool):
            nc.gpsimd.memset(ident[:], 0.0).then_inc(cleared, 1)
            nc.gpsimd.memset(stack2[:], 0.0).then_inc(cleared, 1)
            pool.wait_ge(cleared, 2)
            nc.gpsimd.affine_select(out=ident[:], in_=ident[:], compare_op=ALU.not_equal, fill=1.0, base=0,
                                    pattern=[[-1, P]], channel_multiplier=1).then_inc(ident_made, 1)
            nc.gpsimd.affine_select(out=stack2[:], in_=stack2[:], compare_op=ALU.not_equal, fill=1.0, base=0,
                                    pattern=[[-1, DH]], channel_multiplier=1).then_inc(cleared, 1)
            pool.wait_ge(cleared, 3)
            nc.gpsimd.affine_select(out=stack2[:], in_=stack2[:], compare_op=ALU.not_equal, fill=1.0, base=-DH,
                                    pattern=[[-1, DH]], channel_multiplier=1).then_inc(ident_made, 1)

        idp = (ident, ident_made)
        prepare0(nc, x, x2, q_dram, k_dram, idp, make_ident, sem)
        attend(nc, 0, x, x1_dram, v, mask_dram, idp, stack2, sem, adj=adj, q_dram=q_dram, k_dram=k_dram)
        prepare1(nc, x1_dram, w, a, v1_dram, f1_dram, f2, idp, sem)
        attend(nc, 1, x1_dram, out, v1_dram, mask_dram, idp, stack2, sem, f_dram=f1_dram, f2=f2)


def kernel(x, adj, L0_gnn_x2, L0_gnn_v, L1_gnn_W, L1_gnn_a):
    import numpy as np
    import concourse.bacc as bacc
    from concourse.bass_utils import run_bass_kernel_spmd

    nc = bacc.Bacc("TRN2", target_bir_lowering=False, num_devices=1)
    given = {"x": x, "adj": adj, "x2": L0_gnn_x2, "v": L0_gnn_v, "w": L1_gnn_W, "a": L1_gnn_a}
    arrays = {"in_" + n: np.ascontiguousarray(g) for n, g in given.items()}
    aps = [nc.dram_tensor(n, g.shape, mybir.dt.from_np(g.dtype), kind="ExternalInput").ap() for n, g in arrays.items()]
    out = nc.dram_tensor("out", [N, D], F32, kind="ExternalOutput").ap()
    graph_layers(nc, *aps, out)
    result = run_bass_kernel_spmd(nc, [arrays], core_ids=[0])
    return result.results[0]["out"]
```

```python
from contextlib import ExitStack

import concourse.bass as bass
from concourse import mybir
from concourse.alu_op_type import AluOpType as ALU

ACT = mybir.ActivationFunctionType
F32 = mybir.dt.float32
F32R = mybir.dt.float32r
BF16 = mybir.dt.bfloat16
I32 = mybir.dt.int32
AX = mybir.AxisListType

P = 128
N = 4096
D = 512
H = 8
DH = D // H
NT = N // P
PAIRS = H // 2
SUB = 2
GROUPS = NT // SUB
UNITS = H * GROUPS
V_ALL = UNITS * SUB
HALF = N // 2
QTR = N // 4
BLK = 16
CH = N // P
NEG = -float(2 ** 53)
LOWEST = -3.0e38
EPS = 1e-5
SCALE = DH ** -0.5
ALPHA = 0.2


class Unit:

    def __init__(self, loop, j, made=False, half=None):
        self.loop, self.j, self.made, self.half = loop, j, made, half
        self.fixed = loop + j if isinstance(loop, int) else None

    def at(self, a, b):
        if self.fixed is not None:
            return a * self.fixed + b
        return self.loop * a + (a * self.j + b)

    def exists(self, shift=0):
        return self.fixed is None or 0 <= self.fixed + shift < UNITS

    def has_tile(self, c):
        return self.fixed is None or 0 <= 2 * self.fixed + c < V_ALL

    def turns(self):
        return self.half + (self.j - self.j % 2) // 2 if self.fixed is None else self.fixed // 2

    @property
    def early(self):
        return self.fixed is not None and self.fixed < 2


def tiles(eng, *stages):
    most = max(lag for lag, _ in stages)

    def step(loop, j, half=None):
        for lag, stage in stages:
            if not isinstance(loop, int) or 0 <= loop + j - lag < NT:
                stage(Unit(loop, j - lag, half=half))

    for n in range(4):
        step(n - n % 2, n % 2)
    with eng.Fori(2, NT // 2) as i:
        for j in range(2):
            step(i * 2, j, i)
    for n in range(NT, NT + most):
        step(n - n % 2, n % 2)


def normalise(nc, eng, s, bufs):
    x_all, st, mean, work, rstd = bufs
    for c in range(4):
        eng.wait_ge(s["x_in"][c], 16)
        with eng.Fori(NT // 4 * c, NT // 4 * (c + 1)) as t:
            nc.vector.bn_stats(st[:, t, :], x_all[:, t, :]).then_inc(s["stats"], 1)
    eng.wait_ge(s["stats"], NT)
    n = [0]

    def link(ins):
        n[0] += 1
        ins.then_inc(s["norm"], 1)
        eng.wait_ge(s["norm"], n[0])

    me, ve, mo, vo = (st[:, :, i] for i in (1, 2, 4, 5))
    link(nc.vector.tensor_tensor(mean[:], me, mo, ALU.add))
    link(nc.vector.tensor_scalar(mean[:], mean[:], 0.5, None, ALU.mult))
    link(nc.vector.tensor_tensor(work[:, 0, :], me, mo, ALU.subtract))
    link(nc.vector.tensor_tensor(work[:, 1, :], work[:, 0, :], work[:, 0, :], ALU.mult))
    link(nc.vector.tensor_tensor(work[:, 2, :], ve, vo, ALU.add))
    link(nc.vector.tensor_scalar(work[:, 3, :], work[:, 2, :], 1.0 / D, EPS, ALU.mult, ALU.add))
    nc.vector.scalar_tensor_tensor(out=work[:, 4, :], in0=work[:, 1, :], scalar=0.25, in1=work[:, 3, :],
                                   op0=ALU.mult, op1=ALU.add).then_inc(s["var"], 1)
    eng.wait_ge(s["std"], 1)
    nc.vector.reciprocal(rstd[:], work[:, 5, :]).then_inc(s["rstd"], 1)
    eng.wait_ge(s["rstd"], 1)


def prepare0(nc, x, x2, q_dram, k_dram, ident, make_ident, sem):
    with ExitStack() as ctx:
        sb = lambda name, shape, dt: ctx.enter_context(nc.sbuf_tensor(name, shape, dt))
        x_all = sb("a_x_all", [P, NT, D], F32)
        st = sb("a_st", [P, NT, 6], F32)
        mean = sb("a_mean", [P, NT], F32)
        work = sb("a_work", [P, 6, NT], F32)
        rstd = sb("a_rstd", [P, NT], F32)
        xn = sb("a_xn", [P, 2, D], F32)
        hq = sb("a_hq", [P, 2, D], F32)
        kx = sb("a_kx", [P, 2, D], F32)
        q_st = sb("a_q_st", [P, 2, PAIRS, 2, P], F32R)
        k_st = sb("a_k_st", [P, 2, PAIRS, 2, P], F32R)
        tq = ctx.enter_context(nc.psum_tensor("a_tq", [P, 2, D], F32))
        tk = ctx.enter_context(nc.psum_tensor("a_tk", [P, 2, D], F32))
        s = {n: sem("a_" + n) for n in ("stats", "norm", "var", "std", "rstd", "xn", "h", "tq", "tk", "q_hi",
                                        "q_lo", "k_hi", "k_lo", "passed_pool")}
        s["x_in"] = [sem(f"a_x_in{c}") for c in range(4)]
        k_in = [sem(f"a_k_in{r}") for r in range(2)]
        q_out = [sem(f"a_q_out{r}") for r in range(2)]
        k_out = [[sem(f"a_k_out{r}{e}") for e in range(2)] for r in range(2)]
        x_t = x.rearrange("(t p) d -> p t d", p=P)
        x2_t = x2.rearrange("(t p) d -> t p d", p=P)
        block = ctx.enter_context(nc.Block())

        def store_keys(eng, t, e):
            r = t.j % 2
            for h2 in range(2):
                dst = k_dram.rearrange("(a h) (b d) (t m) -> h b t d a m", h=2, b=2, m=P)[h2, e, t.at(1, 0)]
                eng.dma_start(dst, k_st[DH * h2:DH * h2 + DH, r, :, e, :].bitcast(F32)).then_inc(k_out[r][e], 16)

        @block.sync
        def _(sp):
            for c in range(4):
                sp.dma_start(x_all[:, 8 * c:8 * c + 8, :], x_t[:, 8 * c:8 * c + 8, :]).then_inc(s["x_in"][c], 16)

            def load(t):
                r = t.j % 2
                if not t.early:
                    sp.wait_ge(s["tk"], t.at(1, -1))
                sp.dma_start(kx[:, r, :], x2_t[t.at(1, 0)]).then_inc(k_in[r], 16)

            def store(t):
                r = t.j % 2
                sp.wait_ge(s["k_lo"], t.at(1, 1))
                store_keys(sp, t, 1)
                sp.wait_ge(s["q_lo"], t.at(1, 1))
                sp.dma_start(q_dram[:, t.at(1, 0), :, :, :].rearrange("a p b n -> p a b n"),
                             q_st[:, r].bitcast(F32)).then_inc(q_out[r], 16)

            tiles(sp, (0, load), (2, store))
            for r in range(2):
                sp.wait_ge(q_out[r], 16 * (NT // 2))
                for e in range(2):
                    sp.wait_ge(k_out[r][e], 32 * (NT // 2))

        @block.gpsimd
        def _(pool):
            make_ident(pool)

            def store(t):
                pool.wait_ge(s["k_hi"], t.at(1, 1))
                pool.sem_inc(s["passed_pool"], 1)
                store_keys(pool, t, 0)

            tiles(pool, (0, store))

        @block.vector
        def _(dve):
            normalise(nc, dve, s, (x_all, st, mean, work, rstd))

            def norm(t):
                r = t.j % 2
                if not t.early:
                    dve.wait_ge(s["h"], t.at(1, -1))
                nc.vector.tensor_scalar(xn[:, r, :], x_all[:, t.at(1, 0), :], mean[:, bass.ds(t.at(1, 0), 1)],
                                        rstd[:, bass.ds(t.at(1, 0), 1)], ALU.subtract, ALU.mult).then_inc(s["xn"], 1)

            def low(t):
                r = t.j % 2
                for ps, staged, n in ((tk, k_st, "k"), (tq, q_st, "q")):
                    dve.wait_ge(s[n + "_hi"], t.at(1, 1))
                    nc.vector.tensor_tensor(staged[:, r, :, 1, :], ps[:, r].rearrange("p (a n) -> p a n", n=P),
                                            staged[:, r, :, 0, :], ALU.subtract).then_inc(s[n + "_lo"], 1)

            tiles(dve, (0, norm), (1, low))

        @block.scalar
        def _(act):
            act.wait_ge(s["var"], 1)
            nc.scalar.activation(work[:, 5, :], work[:, 4, :], ACT.Sqrt).then_inc(s["std"], 1)

            def relu(t):
                r = t.j % 2
                act.wait_ge(s["xn"], t.at(1, 1))
                if not t.early:
                    act.wait_ge(s["tq"], t.at(1, -1))
                nc.scalar.activation(hq[:, r, :], xn[:, r, :], ACT.Relu, scale=SCALE).then_inc(s["h"], 1)

            def high(t):
                r = t.j % 2
                for ps, staged, outs, per, n in ((tk, k_st, k_out[r], 32, "k"), (tq, q_st, (q_out[r],), 16, "q")):
                    act.wait_ge(s["t" + n], t.at(1, 1))
                    if not t.early:
                        for out in outs:
                            act.wait_ge(out, t.turns() * per)
                    nc.scalar.activation(staged[:, r, :, 0, :], ps[:, r].rearrange("p (a n) -> p a n", n=P),
                                         ACT.Copy).then_inc(s[n + "_hi"], 1)

            tiles(act, (0, relu), (1, high))

        @block.tensor
        def _(pe):
            pe.wait_ge(ident[1], 2)

            def turn(t):
                r = t.j % 2
                pe.wait_ge(k_in[r], t.turns() * 16 + 16)
                if not t.early:
                    pe.wait_ge(s["k_lo"], t.at(1, -1))
                for a in range(PAIRS):
                    mm = pe.transpose(tk[:, r, a * P:(a + 1) * P], kx[:, r, a * P:(a + 1) * P], ident[0][:])
                mm.then_inc(s["tk"], 1)
                pe.wait_ge(s["h"], t.at(1, 1))
                if not t.early:
                    pe.wait_ge(s["q_lo"], t.at(1, -1))
                for a in range(PAIRS):
                    mm = pe.transpose(tq[:, r, a * P:(a + 1) * P], hq[:, r, a * P:(a + 1) * P], ident[0][:])
                mm.then_inc(s["tq"], 1)

            tiles(pe, (0, turn))


def prepare1(nc, x1, w, a, v_dram, f_dram, part_dram, f2, ident, sem):
    with ExitStack() as ctx:
        sb = lambda name, shape, dt: ctx.enter_context(nc.sbuf_tensor(name, shape, dt))
        x_all = sb("c_x_all", [P, NT, D], F32)
        st = sb("c_st", [P, NT, 6], F32)
        mean = sb("c_mean", [P, NT], F32)
        work = sb("c_work", [P, 6, NT], F32)
        rstd = sb("c_rstd", [P, NT], F32)
        w_sb = sb("c_w", [P, D // P, D], F32)
        a_bc = sb("c_a_bc", [P, 2, D], F32)
        xn = sb("c_xn", [P, 2, D], F32)
        hn = sb("c_hn", [P, 2, D], F32)
        ht = sb("c_ht", [P, 2, D], F32)
        hw_sb = sb("c_hw_sb", [P, 2, D], F32)
        prod = sb("c_prod", [P, 2, 2, D], F32)
        f1 = sb("c_f1", [P, H, NT], F32)
        f_rows = sb("c_f_rows", [P, 2, 2, P], F32)
        parts = sb("c_parts", [P, 3, 2, P], BF16)
        rest = sb("c_rest", [P, 2, 2, P], F32)
        th = ctx.enter_context(nc.psum_tensor("c_th", [P, 2, D], F32))
        hw = ctx.enter_context(nc.psum_tensor("c_hw", [P, 2, D], F32))
        tf = ctx.enter_context(nc.psum_tensor("c_tf", [P, 2, P], F32))
        s = {n: sem("c_" + n) for n in ("stats", "norm", "var", "std", "rstd", "xn", "h", "th", "ht", "hw", "hw_sb",
                                        "prod", "f", "w_in", "a_in", "tf", "f_rows", "parts", "f_out", "f2")}
        s["x_in"] = [sem(f"c_x_in{c}") for c in range(4)]
        v_out = [sem(f"c_v_out{r}") for r in range(2)]
        x_t = x1.rearrange("(t p) d -> p t d", p=P)
        v_t = v_dram.rearrange("(t p) d -> t p d", p=P)
        block = ctx.enter_context(nc.Block())

        @block.sync
        def _(sp):
            for c in range(4):
                sp.dma_start(x_all[:, 8 * c:8 * c + 8, :], x_t[:, 8 * c:8 * c + 8, :]).then_inc(s["x_in"][c], 16)
            for c in range(D // P):
                sp.dma_start(w_sb[:, c, :].rearrange("p (k q) -> p k q", k=H),
                             w[:, c * P:(c + 1) * P, :].rearrange("k f q -> f k q")).then_inc(s["w_in"], 16)
            for e in range(2):
                src = a[:, e * DH:(e + 1) * DH, 0].unsqueeze(0).to_broadcast([P, H, DH])
                sp.dma_start(a_bc[:, e, :].rearrange("p (k q) -> p k q", k=H), src).then_inc(s["a_in"], 16)

            def store(t):
                r = t.j % 2
                sp.wait_ge(s["hw_sb"], t.at(1, 1))
                sp.dma_start(v_t[t.at(1, 0)], hw_sb[:, r, :]).then_inc(v_out[r], 16)

            tiles(sp, (2, store))
            sp.wait_ge(s["f_rows"], 2)
            sp.wait_ge(s["parts"], 5)
            for dst, rows, n in ((f_dram, f_rows, 2), (part_dram, parts, 3)):
                for e in range(n):
                    sp.dma_start(dst[e].rearrange("k (t n) -> (k t) n", n=P).rearrange("(j p) n -> p j n", p=P),
                                 rows[:, e]).then_inc(s["f_out"], 16)
            sp.wait_ge(s["f_out"], 80)
            for r in range(2):
                sp.wait_ge(v_out[r], 16 * (NT // 2))

        @block.vector
        def _(dve):
            normalise(nc, dve, s, (x_all, st, mean, work, rstd))
            dve.wait_ge(s["a_in"], 32)

            def norm(t):
                r = t.j % 2
                if not t.early:
                    dve.wait_ge(s["h"], t.at(1, -1))
                nc.vector.tensor_scalar(xn[:, r, :], x_all[:, t.at(1, 0), :], mean[:, bass.ds(t.at(1, 0), 1)],
                                        rstd[:, bass.ds(t.at(1, 0), 1)], ALU.subtract, ALU.mult).then_inc(s["xn"], 1)

            def dots(t):
                r = t.j % 2
                dve.wait_ge(s["hw_sb"], t.at(1, 1))
                if not t.early:
                    dve.wait_ge(s["f"], t.at(2, -1))
                for e in range(2):
                    nc.vector.tensor_tensor(prod[:, r, e, :], hw_sb[:, r, :], a_bc[:, e, :],
                                            ALU.mult).then_inc(s["prod"], 1)
                f2_v = f2[:].rearrange("p (a g h s) -> p a h g s", a=PAIRS, h=2, s=SUB)
                g = t.turns()
                for e, dst in enumerate((f1[:, :, t.at(1, 0)], f2_v[:, :, :, g, r])):
                    dve.wait_ge(s["prod"], t.at(2, e + 1))
                    src = prod[:, r, e, :]
                    src = (src.rearrange("p (k q) -> p k q", k=H) if e == 0 else
                           src.rearrange("p (a h q) -> p a h q", a=PAIRS, h=2))
                    nc.vector.tensor_reduce(dst, src, AX.X, ALU.add).then_inc(s["f"], 1)

            tiles(dve, (0, norm), (3, dots))
            dve.wait_ge(s["tf"], 1)
            nc.vector.tensor_scalar(f_rows[:, 1], tf[:], ALPHA, None, ALU.mult).then_inc(s["f_rows"], 1)
            nc.vector.tensor_copy(f_rows[:, 0], tf[:]).then_inc(s["f_rows"], 1)
            dve.wait_ge(s["f_rows"], 2)
            left = f_rows[:, 1]
            for i in range(3):
                nc.vector.tensor_copy(parts[:, i], left).then_inc(s["parts"], 1)
                if i < 2:
                    dve.wait_ge(s["parts"], 2 * i + 1)
                    nc.vector.tensor_tensor(rest[:, i], left, parts[:, i], ALU.subtract).then_inc(s["parts"], 1)
                    dve.wait_ge(s["parts"], 2 * i + 2)
                    left = rest[:, i]
            dve.wait_ge(s["f"], 2 * NT)
            nc.vector.tensor_scalar(f2[:], f2[:], ALPHA - 1.0, None, ALU.mult).then_inc(s["f2"], 1)
            dve.wait_ge(s["f2"], 1)

        @block.scalar
        def _(act):
            act.wait_ge(s["var"], 1)
            nc.scalar.activation(work[:, 5, :], work[:, 4, :], ACT.Sqrt).then_inc(s["std"], 1)

            def relu(t):
                r = t.j % 2
                act.wait_ge(s["xn"], t.at(1, 1))
                if not t.early:
                    act.wait_ge(s["th"], t.at(1, -1))
                nc.scalar.activation(hn[:, r, :], xn[:, r, :], ACT.Relu).then_inc(s["h"], 1)

            def copy_h(t):
                r = t.j % 2
                act.wait_ge(s["th"], t.at(1, 1))
                if not t.early:
                    act.wait_ge(s["hw"], t.at(1, -1))
                nc.scalar.activation(ht[:, r, :], th[:, r, :], ACT.Copy).then_inc(s["ht"], 1)

            def copy_hw(t):
                r = t.j % 2
                act.wait_ge(s["hw"], t.at(1, 1))
                if not t.early:
                    act.wait_ge(v_out[r], t.turns() * 16)
                    act.wait_ge(s["prod"], t.at(2, -2))
                nc.scalar.activation(hw_sb[:, r, :], hw[:, r, :], ACT.Copy).then_inc(s["hw_sb"], 1)

            tiles(act, (0, relu), (1, copy_h), (2, copy_hw))

        @block.tensor
        def _(pe):
            pe.wait_ge(s["w_in"], 16 * (D // P))

            def turn(t):
                r = t.j % 2
                pe.wait_ge(s["h"], t.at(1, 1))
                if not t.early:
                    pe.wait_ge(s["ht"], t.at(1, -1))
                for c in range(D // P):
                    mm = pe.transpose(th[:, r, c * P:(c + 1) * P], hn[:, r, c * P:(c + 1) * P], ident[0][:])
                mm.then_inc(s["th"], 1)

            def product(t):
                r = t.j % 2
                pe.wait_ge(s["ht"], t.at(1, 1))
                if not t.early:
                    pe.wait_ge(s["hw_sb"], t.at(1, -1))
                for c in range(D // P):
                    mm = pe.matmul(hw[:, r, :], ht[:, r, c * P:(c + 1) * P], w_sb[:, c, :],
                                   start=(c == 0), stop=(c == D // P - 1))
                mm.then_inc(s["hw"], 1)

            tiles(pe, (0, turn), (1, product))
            pe.wait_ge(s["f"], 2 * NT)
            for j in range(2):
                mm = pe.transpose(tf[:, j, :], f1[:].rearrange("p k t -> p (k t)")[:, j * P:(j + 1) * P], ident[0][:])
            mm.then_inc(s["tf"], 1)


def attend(nc, layer, x_in, x_out, v_dram, mask_dram, ident, stack2, sem, adj=None, q_dram=None, k_dram=None,
           f_dram=None, part_dram=None, f2=None):
    name = "bd"[layer] + "_"
    AK = 8
    M_UNIT = 2 * AK if layer == 0 else 5
    AW = N // 8
    EK, EW = 4, N // 4
    ACT_EVAC = range(1, BLK, 2)
    DVE_EVAC = range(0, BLK, 2) if layer == 0 else ()
    with ExitStack() as ctx:
        sb = lambda n, shape, dt: ctx.enter_context(nc.sbuf_tensor(name + n, shape, dt))
        z = sb("z", [P, 4, N], F32)
        mask = sb("mask", [P, 4, N], BF16)
        v_sb = sb("v", [P, 2, CH, DH], F32)
        pt = sb("pt", [P, 4, 512], F32)
        o_sb = sb("o_sb", [P, 2, 2 * P], F32)
        res = sb("res", [P, 2, SUB, P], F32)
        mx = sb("mx", [P, 8, AK if layer == 0 else 3], F32)
        nm = sb("nm", [P, 8], F32)
        rs = sb("rs", [P, 8, EK], F32)
        rsum = sb("rsum", [P, 2, 2], F32)
        rinv = sb("rinv", [P, 2, 2], F32)
        if layer == 0:
            k_sb = sb("k", [P, 2, N], F32R)
            q_sb = sb("q", [P, 4, 2, P], F32R)
            adj_sb = sb("adj", [P, 2, N], I32)
        else:
            f_bc = sb("f_bc", [P, 2, N], F32)
            f_low = sb("f_low", [P, 2, N - QTR], F32)
            parts = sb("parts", [3, 2, HALF], BF16)
            ident16 = sb("ident16", [P, P], BF16)
            ones16 = sb("ones16", [3, P], BF16)
        t_ps = ctx.enter_context(nc.psum_tensor(name + "t_ps", [P, 4, 512], F32))
        o_ps = ctx.enter_context(nc.psum_tensor(name + "o_ps", [P, 2, 512], F32))
        s_ps = ctx.enter_context(nc.psum_tensor(name + "s_ps", [P, 2, 512], F32))

        s = {n: sem(name + n) for n in (
            "scores", "masked", "max", "exp", "leaky", "turned", "evac_act", "evac_dve", "pv", "o_copied", "o_turned",
            "added", "conv", "sums", "filled", "made16", "passed_dve", "passed_pool")}
        mask_in = [sem(f"{name}mask_in{i}") for i in range(4)]
        mask_out = [sem(f"{name}mask_out{i}") for i in range(4)]
        q_in = [sem(f"{name}q_in{i}") for i in range(4)]
        key_in = [sem(f"{name}key_in{i}") for i in range(2)]
        low_in = [sem(f"{name}low_in{i}") for i in range(2)]
        part_in = [sem(f"{name}part_in{i}") for i in range(2)]
        v_in = [sem(f"{name}v_in{i}") for i in range(2)]
        adj_in = [sem(f"{name}adj_in{i}") for i in range(2)]
        res_in = [sem(f"{name}res_in{i}") for i in range(2)]
        res_out = [sem(f"{name}res_out{i}") for i in range(2)]
        x_g = x_in.rearrange("(g s p) d -> g p s d", s=SUB, p=P)
        y_g = x_out.rearrange("(g s p) d -> g p s d", s=SUB, p=P)
        v_c = v_dram.rearrange("(c p) d -> p c d", p=P)
        LAST = UNITS // 4 - 1
        if layer == 0:
            segments = [("static", -2, 4), ("loop", 1, 7), ("static", 28, 32), ("loop", 8, LAST),
                        ("static", 4 * LAST, UNITS + 1)]
        else:
            segments = [("static", -2, 4), ("loop", 1, LAST), ("static", 4 * LAST, UNITS + 1)]
        UP = 2 * GROUPS

        def f2_of(u, c):
            return f2[:, bass.ds(u.loop * 2 + (2 * u.j + c), 1)]

        def evac_wait(eng, u, b):
            du, b = divmod(b, BLK)
            if not u.exists(du):
                return
            if layer == 1:
                eng.wait_ge(s["evac_act"], u.at(BLK // 2, BLK // 2 * du + b // 2 + 1))
                return
            which, own = ("evac_act", ACT_EVAC) if b in ACT_EVAC else ("evac_dve", DVE_EVAC)
            eng.wait_ge(s[which], u.at(len(own), len(own) * du + own.index(b) + 1))

        def walk(eng, body):
            for kind, a, b in segments:
                if kind == "static":
                    for n in range(a, b):
                        body(Unit(4 * (n // 4), n % 4))
                else:
                    with eng.Fori(a, b) as i:
                        for j in range(4):
                            body(Unit(i * 4, j, made=layer == 0 and a == 1))

        block = ctx.enter_context(nc.Block())

        @block.sync
        def _(sp):
            def load_keys(p, h2):
                if p:
                    last = 4 * GROUPS * p - (3 if h2 == 0 else 1)
                    if layer == 0:
                        sp.wait_ge(s["scores"], AK * (last + 1))
                    else:
                        sp.wait_ge(s["leaky"], 2 * (last + 1))
                        sp.wait_ge(s["filled"], 3 * (last + 1))
                if layer == 0:
                    sp.dma_start(k_sb[:, h2, :].bitcast(F32), k_dram[2 * p + h2]).then_inc(key_in[h2], 16)
                else:
                    k = 2 * p + h2
                    sp.dma_start(parts[:, h2, :], part_dram[:, k, :HALF]).then_inc(part_in[h2], 16)
                    sp.dma_start(f_bc[:, h2, :], f_dram[0, k:k + 1, :].to_broadcast([P, N])).then_inc(key_in[h2], 16)
                    if p == 0 and h2 == 0:
                        load_masks(0, 0, None)
                    sp.dma_start(f_low[:, h2, :], f_dram[1, k:k + 1, QTR:].to_broadcast([P, N - QTR]))\
                        .then_inc(low_in[h2], 16)

            def load_values(p, h2):
                if p:
                    sp.wait_ge(s["pv"], BLK * (UP * p - 1 + h2))
                col = (2 * p + h2) * DH
                sp.dma_start(v_sb[:, h2], v_c[:, :, col:col + DH]).then_inc(v_in[h2], 16)

            def load_queries(p, g, first=False, heads=(0, 1)):
                for i in range(2 * heads[0], 2 * heads[-1] + 2):
                    h2, sub = divmod(i, 2)
                    if not first:
                        sp.wait_ge(s["scores"], g * (4 * AK) + AK * (4 * GROUPS * p + i - 3))
                    src = q_dram[p, g * SUB + sub, DH * h2:DH * h2 + DH].rearrange("d b n -> d (b n)")
                    for half in range(2):
                        sp.dma_start(q_sb[DH * half:DH * half + DH, i].rearrange("d b n -> d (b n)").bitcast(F32),
                                     src).then_inc(q_in[i], 16)

            def load_masks(slot2, g, wait):
                for sub in range(SUB):
                    if wait is not None:
                        sp.wait_ge(s["masked"], wait)
                    sp.dma_start(mask[:, 2 * slot2 + sub, :], mask_dram[g * SUB + sub])\
                        .then_inc(mask_in[2 * slot2 + sub], 16)

            def load_adj(t, sub, first=False):
                if not first:
                    sp.wait_ge(s["conv"], t + (-1))
                sp.dma_start(adj_sb[:, sub, :], adj.rearrange("(t p) m -> t p m", p=P)[t]).then_inc(adj_in[sub], 16)

            def store_rows(p, g, parity):
                sp.wait_ge(s["added"], g * 2 + (UP * p + 2))
                sp.dma_start(y_g[g][:, :, P * p:P * p + P], res[:, parity]).then_inc(res_out[parity], 16)

            def load_rows(p, g, parity, first):
                if not first:
                    sp.wait_ge(res_out[parity], (g - parity) * 8 + 8 * GROUPS * p)
                sp.dma_start(res[:, parity], x_g[g][:, :, P * p:P * p + P]).then_inc(res_in[parity], 16)

            if layer == 0:
                load_adj(0, 0, True)
                load_queries(0, 0, True, heads=(0,))
                load_keys(0, 0)
                load_adj(1, 1, True)
                load_queries(0, 0, True, heads=(1,))
                load_keys(0, 1)
                load_values(0, 0)
                load_values(0, 1)
            else:
                load_keys(0, 0)
                load_keys(0, 1)
                load_values(0, 0)
                load_values(0, 1)
                load_masks(1, 1, None)

            def step(p, g, parity, edge=None):
                made = layer == 0 and p == 0
                last = edge == GROUPS - 1
                if last and p + 1 == PAIRS:
                    pass
                elif last:
                    for i in range(4 if made else 0):
                        sp.wait_ge(mask_out[i], 16 * (GROUPS // 2))
                    load_masks(0, 0, 2 * M_UNIT * (GROUPS * (p + 1) - 1))
                elif made:
                    for sub in range(SUB):
                        load_adj(g * 2 + (2 + sub), sub)
                elif not (edge == 0 and p == 0):
                    load_masks(1 - parity, g + 1, g * (2 * M_UNIT) + 2 * M_UNIT * (GROUPS * p))
                if edge == 0 and p:
                    load_values(p, 0)
                    load_values(p, 1)
                if last and p + 1 < PAIRS:
                    load_keys(p + 1, 0)
                    if layer == 0:
                        load_queries(p + 1, 0, heads=(0,))
                    load_keys(p + 1, 1)
                if edge in (0, 1) and p:
                    store_rows(p - 1, GROUPS - 2 + edge, parity)
                elif edge not in (0, 1):
                    store_rows(p, g - 2, parity)
                load_rows(p, g, parity, first=edge in (0, 1) and p == 0)
                if layer == 0 and not last:
                    load_queries(p, g + 1)
                elif layer == 0 and p + 1 < PAIRS:
                    load_queries(p + 1, 0, heads=(1,))

            for p in range(PAIRS):
                for g in (0, 1):
                    step(p, g, g, edge=g)
                with sp.Fori(1, GROUPS // 2 - 1) as i:
                    for parity in range(2):
                        step(p, i * 2 + parity, parity)
                for g in (GROUPS - 2, GROUPS - 1):
                    step(p, g, g % 2, edge=g)
            for g in (GROUPS - 2, GROUPS - 1):
                store_rows(PAIRS - 1, g, g % 2)
            for parity in range(2):
                sp.wait_ge(res_out[parity], 8 * GROUPS * PAIRS)

        @block.gpsimd
        def _(pool):
            def keep_masks(g, parity):
                for sub in range(SUB):
                    pool.wait_ge(s["conv"], g * 2 + (sub + 1))
                    pool.sem_inc(s["passed_pool"], 1)
                    pool.dma_start(mask_dram[g * SUB + sub], mask[:, 2 * parity + sub, :])\
                        .then_inc(mask_out[2 * parity + sub], 16)

            if layer == 0:
                with pool.Fori(0, GROUPS // 2) as i:
                    for parity in range(2):
                        keep_masks(i * 2 + parity, parity)

        def mask_wait(eng, u, c):
            w = 2 * u.j + c
            slot = 2 * (w % 8 // 4) + w % 2
            if layer == 0 and (u.made if u.fixed is None else 2 * u.fixed + c < 4 * GROUPS):
                eng.wait_ge(s["conv"], u.loop + (2 * (w // 4) + w % 2 + 1))
            else:
                skip = GROUPS // 2 if layer == 0 else 0
                eng.wait_ge(mask_in[slot], u.loop * 4 + 16 * (w // 8 + 1 - skip))

        def masked_count(u, c, k):
            return u.at(M_UNIT, 5 * (c // 2) + 3 * (c % 2) + k)

        @block.tensor
        def _(pe):
            def fill(u, c, k, i):
                if not u.has_tile(c):
                    return
                w = (2 * u.j + c) % 8
                h2, mslot = (w // 2) % 2, 2 * (w // 4) + w % 2
                if i == 0:
                    if k == 0:
                        pe.wait_ge(part_in[h2], (u.at(1, c // 2) // UP) * 16 + 16)
                        mask_wait(pe, u, c)
                    if k or u.fixed is None or 2 * u.fixed + c > 0:
                        pe.wait_ge(s["masked"], masked_count(u, c, 0) + 1 if k else
                                   masked_count(u, c - 1, 1 if c % 2 else 0) + 1)
                cols = slice((2 * k + i) * 512, (2 * k + i + 1) * 512)
                pe.matmul(s_ps[:, i, :], ident16[:], mask[:, mslot, cols], start=True, stop=False)
                pe.matmul(s_ps[:, i, :], ones16[:], parts[:, h2, cols], start=False, stop=True)\
                    .then_inc(s["filled"], 1)

            FILLS = {0: (2, 1, 0), 1: (2, 1, 1), 4: (3, 0, 0), 5: (3, 0, 1), 9: (4, 0, 0), 10: (4, 0, 1)}

            def body(u):
                for b in range(BLK):
                    if layer == 1 and b in FILLS:
                        fill(u, *FILLS[b])
                    if u.exists():
                        if b % 4 == 0:
                            pe.wait_ge(s["exp"], u.at(8, 5 + b // 4))
                        evac_wait(pe, u, b - 4)
                        for i in range(2):
                            for sub in range(SUB):
                                c = 2 * b + i
                                mm = pe.transpose(t_ps[:, b % 4, (2 * i + sub) * P:(2 * i + sub + 1) * P],
                                                  z[:, 2 * (u.j % 2) + sub, c * P:(c + 1) * P], ident[0][:])
                        mm.then_inc(s["turned"], 1)
                    if layer == 0:
                        c, k = (3, b) if b < 8 else (4, b - 8)
                        if u.has_tile(c):
                            v4 = (2 * u.j + c) % 4
                            h2 = v4 // 2
                            if k == 0:
                                pe.wait_ge(q_in[v4], u.loop * 16 + 32 * ((2 * u.j + c) // 4 + 1))
                                pe.wait_ge(key_in[h2], (u.at(1, c // 2) // UP) * 16 + 16)
                            if not (u.fixed is not None and 2 * u.fixed + c == 0 and k < 2):
                                pe.wait_ge(s["masked"], u.at(2 * AK, AK * c + k - 1))
                            for e in range(2):
                                mm = pe.matmul(s_ps[:, k % 2, :], q_sb[:, v4, e, :],
                                               k_sb[:, h2, k * AW:(k + 1) * AW], start=(e == 0), stop=(e == 1))
                            mm.then_inc(s["scores"], 1)
                    du, b2 = divmod(b - 3, BLK)
                    if u.exists(du):
                        h2 = (u.j + du) % 2
                        if b2 == 0:
                            pe.wait_ge(v_in[h2], (u.at(1, du) // UP) * 16 + 16)
                            if u.exists(du - 2):
                                pe.wait_ge(s["added"], u.at(1, du - 1))
                        evac_wait(pe, u, b - 3)
                        for i in range(2):
                            mm = pe.matmul(o_ps[DH * i:DH * i + DH, h2, 0:SUB * P], v_sb[:, h2, 2 * b2 + i, :],
                                           pt[:, b2 % 4, i * 256:(i + 1) * 256], start=(b2 == 0),
                                           stop=(b2 == BLK - 1))
                        mm.then_inc(s["pv"], 1)
                    if b == 5 and u.exists(-1):
                        h2 = (u.j - 1) % 2
                        pe.wait_ge(s["o_copied"], u.at(1, 0))
                        for sub in range(SUB):
                            mm = pe.matmul(o_ps[:, h2, 256 + DH * sub:256 + DH * sub + DH],
                                           o_sb[:, h2, sub * P:(sub + 1) * P], stack2[:], start=True, stop=True,
                                           skip_group_check=True)
                        mm.then_inc(s["o_turned"], 1)

            if layer == 1:
                pe.wait_ge(s["made16"], 2)
            walk(pe, body)

        def copy_out(eng, u, b, own, done):
            du, b = divmod(b, BLK)
            if b not in own or not u.exists(du):
                return
            eng.wait_ge(s["turned"], u.at(BLK, BLK * du + b + 1))
            if not (u.fixed is not None and BLK * (u.fixed + du) + b < 4):
                eng.wait_ge(s["pv"], u.at(BLK, BLK * du + b - 3))
            if done == "evac_act":
                slots = slice(b % 4 - layer, b % 4 + 1)
                nc.scalar.activation(pt[:, slots, :], t_ps[:, slots, :], ACT.Copy).then_inc(s[done], 1)
            else:
                nc.vector.tensor_copy(pt[:, b % 4, :], t_ps[:, b % 4, :]).then_inc(s[done], 1)

        @block.vector
        def _(dve):
            def convert(group, slot, sub, reuse):
                dve.wait_ge(adj_in[sub], group * 16 + 16)
                if reuse is not None:
                    dve.wait_ge(mask_out[slot], reuse)
                nc.vector.tensor_scalar(mask[:, slot, :], adj_sb[:, sub, :], 0, NEG, ALU.is_le,
                                        ALU.mult).then_inc(s["conv"], 1)

            def make_mask(u):
                sub = 0 if u.j % 2 else 1
                if u.fixed is not None:
                    g = (u.fixed + 3 - sub) // 2
                    if u.fixed < -2 or g >= GROUPS or (u.fixed == -2):
                        return
                    convert(g, 2 * (g % 2) + sub, sub, 16 * (g // 2) if g >= 2 else None)
                elif u.made:
                    dg = (u.j + 3 - sub) // 2
                    slot = 2 * (dg % 2) + sub
                    dve.wait_ge(adj_in[sub], u.loop * 8 + (16 * dg + 16))
                    dve.wait_ge(mask_out[slot], u.loop * 4 + 16 * (dg // 2))
                    nc.vector.tensor_scalar(mask[:, slot, :], adj_sb[:, sub, :], 0, NEG, ALU.is_le,
                                            ALU.mult).then_inc(s["conv"], 1)

            def leaky(u, c, k):
                if not u.has_tile(c):
                    return
                v8 = (2 * u.j + c) % 8
                h2 = (v8 // 2) % 2
                first = QTR if c % 2 else HALF
                dve.wait_ge(low_in[h2] if k else key_in[h2], (u.at(1, c // 2) // UP) * 16 + 16)
                if u.fixed is None or 2 * u.fixed + c >= 4:
                    dve.wait_ge(s["turned"], u.at(BLK, BLK * ((c - 4) // 2) + (BLK if k else BLK * first // N)))
                dve.sem_inc(s["passed_dve"], 1)
                if k == 0:
                    nc.vector.tensor_scalar(z[:, v8 % 4, :first], f_bc[:, h2, :first], 1.0 - ALPHA, f2_of(u, c),
                                            ALU.mult, ALU.max).then_inc(s["leaky"], 1)
                else:
                    nc.vector.scalar_tensor_tensor(out=z[:, v8 % 4, first:], in0=f_low[:, h2, first - QTR:],
                                                   scalar=f2_of(u, c), in1=f_bc[:, h2, first:], op0=ALU.add,
                                                   op1=ALU.max).then_inc(s["leaky"], 1)

            def masked_part(u, c, k):
                if not u.has_tile(c):
                    return
                v8 = (2 * u.j + c) % 8
                mslot = 2 * (v8 // 4) + v8 % 2
                quarters = 1 if c % 2 else 2
                dve.wait_ge(s["leaky"], u.at(4, 2 * c + (2 if k == quarters else 1)))
                if k == quarters:
                    mask_wait(dve, u, c)
                    cols, add = slice(k * QTR, N), mask[:, mslot, k * QTR:]
                else:
                    dve.wait_ge(s["filled"], u.at(6, 6 * (c // 2) + 4 * (c % 2) + 2 * k + 2))
                    cols, add = slice(k * QTR, (k + 1) * QTR), s_ps[:].rearrange("p b n -> p (b n)")
                dve.sem_inc(s["passed_dve"], 1)
                nc.vector.tensor_tensor_reduce(
                    out=z[:, v8 % 4, cols], in0=z[:, v8 % 4, cols], in1=add, scale=1.0, scalar=LOWEST, op0=ALU.add,
                    op1=ALU.max, accum_out=mx[:, v8, k:k + 1]).then_inc(s["masked"], 1)

            def masked(u, c, k):
                if not u.has_tile(c):
                    return
                v8 = (2 * u.j + c) % 8
                sub, h2 = v8 % 2, (v8 // 2) % 2
                mslot = 2 * (v8 // 4) + sub
                late = u.fixed is None or 2 * u.fixed + c >= 4
                if k == 0:
                    mask_wait(dve, u, c)
                dve.wait_ge(s["scores"], u.at(2 * AK, AK * c + k + 1))
                if late:
                    blocks = BLK // AK * (k + 1)
                    dve.wait_ge(s["turned"], u.at(BLK, BLK * ((c - 4) // 2) + blocks))
                dve.sem_inc(s["passed_dve"], 1)
                nc.vector.tensor_tensor_reduce(
                    out=z[:, v8 % 4, k * AW:(k + 1) * AW], in0=s_ps[:, k % 2, :],
                    in1=mask[:, mslot, k * AW:(k + 1) * AW],
                    scale=1.0, scalar=LOWEST, op0=ALU.add, op1=ALU.max,
                    accum_out=mx[:, v8, k:k + 1]).then_inc(s["masked"], 1)

            def maximum(u, c):
                if not u.has_tile(c):
                    return
                v8 = (2 * u.j + c) % 8
                n = AK if layer == 0 else 2 if c % 2 else 3
                dve.wait_ge(s["masked"], u.at(2 * AK, AK * (c + 1)) if layer == 0 else masked_count(u, c, n))
                nc.vector.tensor_reduce(nm[:, v8:v8 + 1], mx[:, v8, :n], AX.X, ALU.max,
                                        negate=True).then_inc(s["max"], 1)

            def add_up(u):
                if not u.exists(-1):
                    return
                h2 = (u.j - 1) % 2
                v8 = (2 * u.j - 2) % 8
                parity = ((u.j - 1) % 4) // 2
                dve.wait_ge(s["exp"], u.at(8, 0))
                nc.vector.tensor_reduce(rsum[:, h2, :], rs[:, v8:v8 + 2, :], AX.X, ALU.add).then_inc(s["sums"], 1)
                dve.wait_ge(s["sums"], u.at(2, -1))
                nc.vector.reciprocal(rinv[:, h2, :], rsum[:, h2, :]).then_inc(s["sums"], 1)
                dve.wait_ge(s["sums"], u.at(2, 0))
                dve.wait_ge(res_in[parity], u.loop * 4 + 16 * ((u.j - 1) // 4 + 1))
                dve.wait_ge(s["o_turned"], u.at(1, 0))
                for sub in range(SUB):
                    r = res[:, parity, sub, DH * h2:DH * h2 + DH]
                    ins = nc.vector.scalar_tensor_tensor(
                        out=r, in0=o_ps[:, h2, 256 + DH * sub:256 + DH * sub + DH], scalar=rinv[:, h2, sub:sub + 1],
                        in1=r, op0=ALU.mult, op1=ALU.add)
                ins.then_inc(s["added"], 1)

            STEPS = {0: ((masked_part, 3, 0),), 1: ((leaky, 3, 1),), 4: ((leaky, 4, 0),), 5: ((masked_part, 3, 1),),
                     8: ((masked_part, 4, 0),), 9: ((leaky, 4, 1),), 11: ((masked_part, 4, 1),), 12: ((leaky, 5, 0),),
                     13: ((masked_part, 4, 2),)}

            def body(u):
                for b in range(BLK):
                    copy_out(dve, u, b - 1, DVE_EVAC, "evac_dve")
                    if layer == 0:
                        masked(u, *((3, b) if b < 8 else (4, b - 8)))
                    for step, c, k in STEPS.get(b, ()) if layer == 1 else ():
                        step(u, c, k)
                    if b == 0:
                        maximum(u, 2)
                    if b == (8, 6)[layer]:
                        maximum(u, 3)
                    if b == 7:
                        add_up(u)
                    if layer == 0 and b == 3:
                        make_mask(u)
                    if layer == 0 and b == BLK - 1 and u.fixed == -2:
                        convert(0, 1, 1, None)

            if layer == 0:
                convert(0, 0, 0, None)
            if layer == 1:
                nc.vector.tensor_copy(ident16[:], ident[0][:]).then_inc(s["made16"], 1)
                nc.vector.memset(ones16[:], 1.0).then_inc(s["made16"], 1)
            walk(dve, body)

        @block.scalar
        def _(act):
            def tile_chunk(n):
                n += 3 - 2 * layer
                return (1 + n // 4, n % 4)

            def exp(u, c, e):
                if not u.has_tile(c):
                    return
                v8 = (2 * u.j + c) % 8
                if e == 0:
                    act.wait_ge(s["max"], u.at(2, c + 1))
                    if u.fixed is None or 2 * u.fixed + c >= 8:
                        act.wait_ge(s["added"], u.at(1, c // 2 - 3))
                zc = z[:, v8 % 4, e * EW:(e + 1) * EW]
                nc.scalar.activation(zc, zc, ACT.Exp, bias=nm[:, v8:v8 + 1],
                                     accum_out=rs[:, v8, e:e + 1]).then_inc(s["exp"], 1)

            def copy_o(u):
                if not u.exists(-1):
                    return
                h2 = (u.j - 1) % 2
                act.wait_ge(s["pv"], u.at(BLK, 0))
                if u.exists(-3):
                    act.wait_ge(s["o_turned"], u.at(1, -2))
                nc.scalar.activation(o_sb[:, h2, :], o_ps[:, h2, 0:SUB * P], ACT.Copy).then_inc(s["o_copied"], 1)

            def body(u):
                for b in range(BLK):
                    copy_out(act, u, b - 1, ACT_EVAC, "evac_act")
                    if b == 3:
                        copy_o(u)
                    if b % 2 == layer:
                        exp(u, *tile_chunk(b // 2))

            walk(act, body)


def graph_layers(nc, x, adj, x2, v, w, a, out):
    with ExitStack() as ctx:
        def sem(name):
            return ctx.enter_context(nc.semaphore(name))

        ident = ctx.enter_context(nc.sbuf_tensor("ident", [P, P], F32))
        stack2 = ctx.enter_context(nc.sbuf_tensor("stack2", [P, DH], F32))
        f2 = ctx.enter_context(nc.sbuf_tensor("f2", [P, V_ALL], F32))
        ident_made = sem("ident_made")
        q_dram = nc.dram_tensor("q_parts", [PAIRS, NT, P, 2, P], F32, kind="Internal").ap()
        k_dram = nc.dram_tensor("k_parts", [H, P, N], F32, kind="Internal").ap()
        mask_dram = nc.dram_tensor("masks", [NT, P, N], BF16, kind="Internal").ap()
        x1_dram = nc.dram_tensor("x1", [N, D], F32, kind="Internal").ap()
        v1_dram = nc.dram_tensor("v1", [N, D], F32, kind="Internal").ap()
        f1_dram = nc.dram_tensor("f1", [2, H, N], F32, kind="Internal").ap()
        part_dram = nc.dram_tensor("f1_parts", [3, H, N], BF16, kind="Internal").ap()
        cleared = sem("ident_cleared")

        def make_ident(pool):
            nc.gpsimd.memset(ident[:], 0.0).then_inc(cleared, 1)
            nc.gpsimd.memset(stack2[:], 0.0).then_inc(cleared, 1)
            pool.wait_ge(cleared, 2)
            nc.gpsimd.affine_select(out=ident[:], in_=ident[:], compare_op=ALU.not_equal, fill=1.0, base=0,
                                    pattern=[[-1, P]], channel_multiplier=1).then_inc(ident_made, 1)
            nc.gpsimd.affine_select(out=stack2[:], in_=stack2[:], compare_op=ALU.not_equal, fill=1.0, base=0,
                                    pattern=[[-1, DH]], channel_multiplier=1).then_inc(cleared, 1)
            pool.wait_ge(cleared, 3)
            nc.gpsimd.affine_select(out=stack2[:], in_=stack2[:], compare_op=ALU.not_equal, fill=1.0, base=-DH,
                                    pattern=[[-1, DH]], channel_multiplier=1).then_inc(ident_made, 1)

        idp = (ident, ident_made)
        prepare0(nc, x, x2, q_dram, k_dram, idp, make_ident, sem)
        attend(nc, 0, x, x1_dram, v, mask_dram, idp, stack2, sem, adj=adj, q_dram=q_dram, k_dram=k_dram)
        prepare1(nc, x1_dram, w, a, v1_dram, f1_dram, part_dram, f2, idp, sem)
        attend(nc, 1, x1_dram, out, v1_dram, mask_dram, idp, stack2, sem, f_dram=f1_dram,
               part_dram=part_dram, f2=f2)


def kernel(x, adj, L0_gnn_x2, L0_gnn_v, L1_gnn_W, L1_gnn_a):
    import numpy as np
    import concourse.bacc as bacc
    from concourse.bass_utils import run_bass_kernel_spmd

    nc = bacc.Bacc("TRN2", target_bir_lowering=False, num_devices=1)
    given = {"x": x, "adj": adj, "x2": L0_gnn_x2, "v": L0_gnn_v, "w": L1_gnn_W, "a": L1_gnn_a}
    arrays = {"in_" + n: np.ascontiguousarray(g) for n, g in given.items()}
    aps = [nc.dram_tensor(n, g.shape, mybir.dt.from_np(g.dtype), kind="ExternalInput").ap() for n, g in arrays.items()]
    out = nc.dram_tensor("out", [N, D], F32, kind="ExternalOutput").ap()
    graph_layers(nc, *aps, out)
    result = run_bass_kernel_spmd(nc, [arrays], core_ids=[0])
    return result.results[0]["out"]
```
